# Optimizing a Trainium2 kernel written in Bass

```python
import numpy as np
import jax
import jax.numpy as jnp

def _softmax(x, axis=-1):
    return jax.nn.softmax(x, axis=axis)

def _gelu(x):
    return jax.nn.gelu(x, approximate=True)

def _silu(x):
    return jax.nn.silu(x)

def _sigmoid(x):
    return jax.nn.sigmoid(x)

def _layernorm(x, axis=-1, eps=1e-05):
    m = jnp.mean(x, axis=axis, keepdims=True)
    v = jnp.var(x, axis=axis, keepdims=True)
    return (x - m) / jnp.sqrt(v + eps)

def _scatter_add(tgt, idx, src, axis=0):
    return tgt.at[idx].add(src)

def _segment_sum(src, seg, n):
    return jax.ops.segment_sum(src, seg, n)
kernel_name = 'mk_gnn_resnorm_d1_gnn_r8_54836d'

def setup_inputs(seed: int=0):
    np.random.seed(seed)
    _w = jnp.asarray

    def _rec_inputs():
        import jax
        import jax.numpy as jnp
        _gk = jax.random.key(seed)
        x = -0.000202 + 1 * jax.random.normal(jax.random.fold_in(_gk, 1), (12500, 128), jnp.float32)
        src = jax.random.randint(jax.random.fold_in(_gk, 2), (400000,), 0, 12500, jnp.int32)
        dst = jax.random.randint(jax.random.fold_in(_gk, 3), (400000,), 0, 12500, jnp.int32)
        _o = jnp.argsort(dst, stable=True)
        src = src[_o]
        dst = dst[_o]
        edge_attr_3 = -0.000451519 + 1.00018 * jax.random.normal(jax.random.fold_in(_gk, 12), (400000, 3), jnp.float32)
        edge_weight = jax.random.uniform(jax.random.fold_in(_gk, 13), (400000,), jnp.float32, 0.0, 0.999998)
        return (x, src, dst, edge_attr_3, edge_weight)
    x, src, dst, edge_attr_3, edge_weight = _rec_inputs()

    def _L0_gnn_setup():
        import jax, jax.numpy as jnp
        import numpy as np
        N = 6250
        E = 100000
        MUL = 32
        NB = 8
        R_MAX = 1.0
        AVG = 16.0
        SQ3 = 3.0 ** 0.5

        def _radial_embedding(r):
            x = jnp.clip(r / R_MAX, 0.0, 1.0)
            centers = jnp.arange(NB, dtype=jnp.float32) / (NB - 1)
            sigma = 1.0 / (NB - 1)
            emb = jnp.exp(-0.5 * ((x[:, None] - centers[None, :]) / sigma) ** 2)
            emb = emb * NB ** 0.5 * (r <= R_MAX).astype(jnp.float32)[:, None]
            return emb
        key = jax.random.key(seed)
        k = jax.random.split(key, 12)
        inp = {'node_feats': jax.random.normal(k[0], (N, 4 * MUL), dtype=jnp.float32), 'edge_vec': jax.random.normal(k[1], (E, 3), dtype=jnp.float32), 'edge_length': jax.random.uniform(k[2], (E,), dtype=jnp.float32), 'senders': jax.random.randint(k[3], (E,), 0, N, dtype=jnp.int32), 'receivers': jax.random.randint(k[4], (E,), 0, N, dtype=jnp.int32), 'num_nodes': N, 'W_up0': jax.random.normal(k[5], (MUL, MUL), dtype=jnp.float32), 'W_up1': jax.random.normal(k[6], (MUL, MUL), dtype=jnp.float32), 'mlp_w0': jax.random.normal(k[7], (NB, 64), dtype=jnp.float32) / NB ** 0.5, 'mlp_b0': jnp.zeros((64,), dtype=jnp.float32), 'mlp_w1': jax.random.normal(k[8], (64, 64), dtype=jnp.float32) / 8.0, 'mlp_b1': jnp.zeros((64,), dtype=jnp.float32), 'mlp_w2': jax.random.normal(k[9], (64, 4 * MUL), dtype=jnp.float32) / 8.0, 'mlp_b2': jnp.zeros((4 * MUL,), dtype=jnp.float32), 'W_out0': jax.random.normal(k[10], (2 * MUL, MUL), dtype=jnp.float32), 'W_out1': jax.random.normal(k[11], (2 * MUL, MUL), dtype=jnp.float32)}
        return inp
    _L0_gnn_all = _L0_gnn_setup()
    _L0_gnn_in = {k: v for k, v in _L0_gnn_all.items() if k in ('W_up0', 'W_up1', 'mlp_w0', 'mlp_b0', 'mlp_w1', 'mlp_b1', 'mlp_w2', 'mlp_b2', 'W_out0', 'W_out1')}
    del _L0_gnn_all
    return {'x': x, 'src': src, 'dst': dst, 'edge_attr_3': edge_attr_3, 'edge_weight': edge_weight, 'L0_gnn_W_up0': _L0_gnn_in['W_up0'], 'L0_gnn_W_up1': _L0_gnn_in['W_up1'], 'L0_gnn_mlp_w0': _L0_gnn_in['mlp_w0'], 'L0_gnn_mlp_b0': _L0_gnn_in['mlp_b0'], 'L0_gnn_mlp_w1': _L0_gnn_in['mlp_w1'], 'L0_gnn_mlp_b1': _L0_gnn_in['mlp_b1'], 'L0_gnn_mlp_w2': _L0_gnn_in['mlp_w2'], 'L0_gnn_mlp_b2': _L0_gnn_in['mlp_b2'], 'L0_gnn_W_out0': _L0_gnn_in['W_out0'], 'L0_gnn_W_out1': _L0_gnn_in['W_out1']}

def reference(x, src, dst, edge_attr_3, edge_weight, L0_gnn_W_up0, L0_gnn_W_up1, L0_gnn_mlp_w0, L0_gnn_mlp_b0, L0_gnn_mlp_w1, L0_gnn_mlp_b1, L0_gnn_mlp_w2, L0_gnn_mlp_b2, L0_gnn_W_out0, L0_gnn_W_out1):
    import jax
    import jax.numpy as jnp

    def _L0_gnn_ref(node_feats, edge_vec, edge_length, senders, receivers, num_nodes, W_up0, W_up1, mlp_w0, mlp_b0, mlp_w1, mlp_b1, mlp_w2, mlp_b2, W_out0, W_out1):
        import jax, jax.numpy as jnp
        import numpy as np
        N = 6250
        E = 100000
        MUL = 32
        NB = 8
        R_MAX = 1.0
        AVG = 16.0
        SQ3 = 3.0 ** 0.5

        def _radial_embedding(r):
            x = jnp.clip(r / R_MAX, 0.0, 1.0)
            centers = jnp.arange(NB, dtype=jnp.float32) / (NB - 1)
            sigma = 1.0 / (NB - 1)
            emb = jnp.exp(-0.5 * ((x[:, None] - centers[None, :]) / sigma) ** 2)
            emb = emb * NB ** 0.5 * (r <= R_MAX).astype(jnp.float32)[:, None]
            return emb
        f32 = jnp.float32
        rhat = edge_vec / (jnp.linalg.norm(edge_vec, axis=-1, keepdims=True) + 1e-12)
        Y1 = SQ3 * rhat
        emb = _radial_embedding(edge_length)
        h = jax.nn.silu(emb @ mlp_w0 + mlp_b0)
        h = jax.nn.silu(h @ mlp_w1 + mlp_b1)
        w = (h @ mlp_w2 + mlp_b2).reshape(-1, 4, MUL)
        s = node_feats[:, :MUL]
        v = node_feats[:, MUL:].reshape(-1, MUL, 3)
        xs = s @ W_up0 / f32(MUL) ** 0.5
        xv = jnp.einsum('nmc,mk->nkc', v, W_up1) / f32(MUL) ** 0.5
        ss = xs[senders]
        vv = xv[senders]
        m0 = w[:, 0] * ss
        m1 = w[:, 1][:, :, None] * ss[:, :, None] * Y1[:, None, :]
        m2 = w[:, 2][:, :, None] * vv
        m3 = w[:, 3] * (jnp.einsum('emc,ec->em', vv, Y1) / SQ3)
        mid_s = jnp.concatenate([m0, m3], axis=1)
        mid_v = jnp.concatenate([m1, m2], axis=1)
        msg_s = jax.ops.segment_sum(mid_s, receivers, num_segments=num_nodes)
        msg_v = jax.ops.segment_sum(mid_v, receivers, num_segments=num_nodes)
        out_s = msg_s @ W_out0 / f32(2 * MUL) ** 0.5
        out_v = jnp.einsum('nmc,mk->nkc', msg_v, W_out1) / f32(2 * MUL) ** 0.5
        out = jnp.concatenate([out_s, out_v.reshape(-1, 3 * MUL)], axis=1)
        return out / max(AVG, 1e-08)
    x = _layernorm(x + _L0_gnn_ref(x, edge_attr_3, edge_weight, src, dst, 12500, L0_gnn_W_up0, L0_gnn_W_up1, L0_gnn_mlp_w0, L0_gnn_mlp_b0, L0_gnn_mlp_w1, L0_gnn_mlp_b1, L0_gnn_mlp_w2, L0_gnn_mlp_b2, L0_gnn_W_out0, L0_gnn_W_out1), axis=-1)
    return x

_drawn_inputs = setup_inputs


def setup_inputs(seed=0):
    import zlib

    import numpy as np

    out = dict(_drawn_inputs(seed))
    spreads = {'L0_gnn_mlp_b0': (0.0, 0.607), 'L0_gnn_mlp_b1': (0.0, 0.416), 'L0_gnn_mlp_b2': (0.0, 0.1)}
    factors = {}
    for name, (base, spread) in spreads.items():
        noise = np.random.default_rng([zlib.crc32(name.encode()), seed]).standard_normal(out[name].shape)
        drawn = base * np.exp(spread * noise) if base else spread * noise
        out[name] = jnp.asarray(drawn.astype(out[name].dtype))
    for name, factor in factors.items():
        out[name] = (out[name] * factor).astype(out[name].dtype)
    return out
```

```python
import math
from contextlib import ExitStack

import concourse.bass as bass
from concourse import mybir

F32 = mybir.dt.float32
BF16 = mybir.dt.bfloat16
I32 = mybir.dt.int32
ALU = mybir.AluOpType
ACT = mybir.ActivationFunctionType
AX = mybir.AxisListType

P = 128
NODES, EDGES, FEAT, MUL, CENTERS, HID = 12500, 400000, 128, 32, 8, 64
T = 14
V = 2 * T
HALF_V = V // 2
SUB = T * P
CHUNK = 2 * SUB
EDGE_TILES = EDGES // P
CHUNKS = -(-EDGE_TILES // V)
LAST_B = EDGE_TILES - (CHUNKS - 1) * V - T
WINDOW = 64
GROUP = CHUNK // 16
HCOL = 2 * GROUP
BLOCKS = 9
MSG = 256
NODE_TILES = -(-NODES // P)
LAST_NODES = NODES - (NODE_TILES - 1) * P
NG = 4
NODE_GROUPS = NODE_TILES // NG
SHORT = NODE_TILES - NODE_GROUPS * NG
RING = 4
LG = 14
assert LAST_B == 3 and CHUNKS % 2 == 0 and NODE_GROUPS % RING == 0 and NODE_TILES % LG == 0


def spread(ap, axis, n):
    shape = list(ap.shape)
    shape.insert(axis, n)
    return ap.unsqueeze(axis).broadcast_to(shape)


def build(nc, x, src, dst, edge_attr_3, edge_weight, W_up0, W_up1, mlp_w0, mlp_b0, mlp_w1, mlp_b1,
          mlp_w2, mlp_b2, W_out0, W_out1, out):
    src2 = src.rearrange("(t p) -> t p", p=P)
    dst2 = dst.rearrange("(t p) -> t p", p=P)
    attr2 = edge_attr_3.rearrange("(t p) c -> t (p c)", p=P)
    dst_flat = dst.rearrange("(a n) -> a n", a=1)
    r_flat = edge_weight

    ctx = ExitStack()
    with ctx:
        def sb(name, shape, dt=F32):
            return ctx.enter_context(nc.sbuf_tensor(name, shape, dt))

        def ps(name, shape=(P, 512)):
            return ctx.enter_context(nc.psum_tensor(name, list(shape), F32))

        def sem(name):
            return ctx.enter_context(nc.semaphore(name))

        table = nc.dram_tensor("projected", (NODES, FEAT), F32).ap()
        node_sum = nc.dram_tensor("node_sum", (NODES + P, FEAT), F32).ap()
        leftover = nc.dram_tensor("leftover", (EDGE_TILES, P), I32).ap()

        iota_i = sb("iota_i", [P, P], I32)
        pcol_i = sb("pcol_i", [P, 3], I32)
        iota_f = sb("iota_f", [P, P])
        trash_row = sb("trash_row", [P, P])
        pcol = sb("pcol", [P, 1])
        window_lane = sb("window_lane", [P, 1])
        minus_center = sb("minus_center", [P, 1])
        ident = sb("ident", [P, P])
        group_rep = sb("group_rep", [P, P])
        group_low = sb("group_low", [P, P])
        row_select = sb("row_select", [P, V])
        w0_rep = sb("w0_rep", [P, HID])
        w0_wide = sb("w0_wide", [P, 8, 2, HID])
        w0_keep = sb("w0_keep", [P, 8, 2, HID])
        w0_groups = sb("w0_groups", [P, 8, 2, HID])
        w1_diag = sb("w1_diag", [P, P])
        w2_diag = sb("w2_diag", [P, 2 * P])
        bias01 = sb("bias01", [P, 2])
        b2_rep = sb("b2_rep", [P, P])
        b2_part = sb("b2_part", [P, 3, P], BF16)
        b2_rest = sb("b2_rest", [P, 2, P])
        b2_mask = sb("b2_mask", [P, 3])
        b2_sum = sb("b2_sum", [P, 2, P])
        b2_rows = sb("b2_rows", [P, 4, P], BF16)
        ones_bf = sb("ones_bf", [P, P], BF16)
        wup_raw = sb("wup_raw", [P, P])
        wup = sb("wup", [P, P])
        wout_raw = sb("wout_raw", [P, 2, MUL])
        wout_scale = sb("wout_scale", [P, 2])
        wout = sb("wout", [P, 2, P])
        zeros = sb("zeros", [P, P])

        x_ring = sb("x_ring", [P, RING, NG, P])
        xT = sb("xT", [P, 2, NG * P])
        proj = sb("proj", [P, 2, NG * P])

        src_row = [sb(f"src_row{b}", [P, P], I32) for b in range(2)]
        dst_row = [sb(f"dst_row{b}", [P, P], I32) for b in range(2)]
        attr_row = [sb(f"attr_row{b}", [P, P, 3]) for b in range(2)]
        base = [sb(f"base{b}", [P, 2], I32) for b in range(2)]
        r_in = [sb(f"r_in{b}", [P, GROUP]) for b in range(2)]
        src_f = sb("src_f", [P, P])
        rel = sb("rel", [P, P])
        window_out = sb("window_out", [P, P])
        chunk_rel = sb("chunk_rel", [P, P])
        chunk_out = sb("chunk_out", [P, P])
        missed = sb("missed", [P, P])
        missed_any = sb("missed_any", [P, P])
        above_trash = sb("above_trash", [P, P])
        missed_row = sb("missed_row", [P, P])
        left_row = [sb(f"left_row{b}", [P, P], I32) for b in range(2)]
        window_node = [sb(f"window_node{b}", [P, 1]) for b in range(2)]
        idx = [sb(f"idx{b}", [P, V], I32) for b in range(2)]
        one_hot = [sb(f"one_hot{b}", [P, V, WINDOW]) for b in range(2)]
        square = sb("square", [P, 3, V])
        norm_a = sb("norm_a", [P, V])
        norm2 = sb("norm2", [P, V])
        norm = sb("norm", [P, V])
        norm_eps = sb("norm_eps", [P, V])
        norm_inv = sb("norm_inv", [P, V])
        unit = [sb(f"unit{b}", [P, 3, V]) for b in range(2)]

        r_clip = sb("r_clip", [P, GROUP])
        gauss_arg = sb("gauss_arg", [P, GROUP])
        gauss = sb("gauss", [P, GROUP])
        emb = sb("emb", [P, GROUP])
        h1 = sb("h1", [P, SUB])
        h2 = [sb(f"h2_{b}", [P, SUB]) for b in range(2)]
        w_edge = [sb(f"w_edge{h}", [P, HALF_V, P]) for h in range(2)]

        rows = [[sb(f"rows{b}{h}", [P, HALF_V, FEAT]) for h in range(2)] for b in range(2)]
        msg = [sb(f"msg{h}", [P, HALF_V, BLOCKS * MUL]) for h in range(2)]
        dot = sb("dot", [P, HALF_V, 3, MUL])
        dot_a = sb("dot_a", [P, HALF_V, MUL])
        dot_b = sb("dot_b", [P, HALF_V, MUL])

        place = [sb(f"place{b}", [P, P]) for b in range(2)]
        win_sb = sb("win_sb", [P, MSG])
        nodesT = sb("nodesT", [P, MSG])
        old_sum = sb("old_sum", [P, P])
        new_sum = sb("new_sum", [P, P])

        one_src = sb("one_src", [P, 1], I32)
        one_left = sb("one_left", [P, 1], I32)
        one_attr = sb("one_attr", [P, 3])
        one_square = sb("one_square", [P, 3])
        one_norm = sb("one_norm", [P, 5])
        one_unit = sb("one_unit", [P, 3])
        recv = sb("recv", [P, 1])
        recv_diag = sb("recv_diag", [P, P])
        same = sb("same", [P, P])
        same_earlier = sb("same_earlier", [P, P])
        earlier = sb("earlier", [P, P])
        repeated = sb("repeated", [P, 3])
        target = sb("target", [P, 1], I32)
        ones = sb("ones", [P, P])
        valid_row = sb("valid_row", [P, 1])
        missed_col = sb("missed_col", [P, 2])
        flag = sb("flag", [1, 1], I32)

        assert LG == HALF_V
        ln_in = [rows[b][0] for b in range(2)]
        ln_out = [rows[b][1] for b in range(2)]
        ln_mid = w_edge[0]
        ln_stat = sb("ln_stat", [P, LG, 6])
        ln_mv = sb("ln_mv", [P, 2, LG, 2])
        ln_sd = sb("ln_sd", [P, LG])
        ln_rs = sb("ln_rs", [P, LG])
        ln_mrs = sb("ln_mrs", [P, LG])
        ln_eps = sb("ln_eps", [P, LG])

        hid_ps = [ps(f"hid_ps{i}") for i in range(2)]
        w_ps = [ps(f"w_ps{i}") for i in range(2)]
        row_ps = ps("row_ps")
        win_ps = ps("win_ps")
        upd_ps = ps("upd_ps")

        const_loaded = sem("const_loaded")
        const_pool = sem("const_pool")
        const_step = sem("const_step")
        x_loaded = [sem(f"x_loaded{i}") for i in range(RING)]
        x_saved = [sem(f"x_saved{i}") for i in range(RING)]
        pad_saved = sem("pad_saved")
        xT_ready = sem("xT_ready")
        xT_copied = sem("xT_copied")
        proj_ready = sem("proj_ready")
        proj_copied = sem("proj_copied")
        proj_saved = [sem(f"proj_saved{i}") for i in range(2)]
        rows_loaded = [sem(f"rows_loaded{b}") for b in range(2)]
        rows_ready = sem("rows_ready")
        edge_scalars = sem("edge_scalars")
        clip_ready = sem("clip_ready")
        gauss_step = sem("gauss_step")
        emb_ready = sem("emb_ready")
        left_step = sem("left_step")
        left_ready = sem("left_ready")
        left_saved = [sem(f"left_saved{b}") for b in range(2)]
        transposed = sem("transposed")
        squared = sem("squared")
        norm_step = sem("norm_step")
        norm2_ready = sem("norm2_ready")
        norm_ready = sem("norm_ready")
        idx_ready = sem("idx_ready")
        one_hot_ready = sem("one_hot_ready")
        unit_ready = sem("unit_ready")
        rows_free = sem("rows_free")
        gathered = [[sem(f"gathered{b}{h}") for h in range(2)] for b in range(2)]
        hid_ready = sem("hid_ready")
        hid_copied = sem("hid_copied")
        w_ready = sem("w_ready")
        w_copied = sem("w_copied")
        msg_step = sem("msg_step")
        msg_ready = sem("msg_ready")
        msg_summed = sem("msg_summed")
        win_copied = sem("win_copied")
        place_ready = sem("place_ready")
        placed = sem("placed")
        placed_copied = sem("placed_copied")
        upd_ready = sem("upd_ready")
        window_read = sem("window_read")
        window_added = sem("window_added")
        window_saved = sem("window_saved")
        flag_step = sem("flag_step")
        flag_summed = sem("flag_summed")
        flag_ready = sem("flag_ready")
        tile_loaded = sem("tile_loaded")
        tile_vector = sem("tile_vector")
        tile_scalar = sem("tile_scalar")
        tile_tensor = sem("tile_tensor")
        tile_rows = sem("tile_rows")
        tile_sums = sem("tile_sums")
        tile_saved = sem("tile_saved")
        tile_done = sem("tile_done")
        norm_loaded = [sem(f"norm_loaded{i}") for i in range(2)]
        ln_step = sem("ln_step")
        ln_var = sem("ln_var")
        ln_std = sem("ln_std")
        ln_ready = sem("ln_ready")
        out_saved = [sem(f"out_saved{i}") for i in range(2)]

        LOADS_PER = 10
        n_const = {}

        def each_chunk(eng, body):
            for c in (0, 1):
                body(c // 2, c % 2, c)
            with eng.Fori(1, CHUNKS // 2 - 2) as k:
                body(k, 0, None)
                body(k, 1, None)
            for c in range(CHUNKS - 4, CHUNKS):
                body(c // 2, c % 2, c)

        def after(k, b, steps=1):
            return (k + (b + steps) // 2, (b + steps) % 2)

        def from_chunk(at, n):
            return at is None or at >= n

        def has_next(at, steps=1):
            return at is None or at + steps < CHUNKS

        def loaded_count(k, at):
            return 16 * LOADS_PER * (k + 1) + (16 if at == CHUNKS - 1 else 0)

        def sub_rows(b_tiles):
            return ((0, 0, T), (WINDOW, T, b_tiles))

        def last_tiles(at, h):
            return [v for v in range(h * HALF_V, (h + 1) * HALF_V)
                    if at != CHUNKS - 1 or v % 2 == 0 or v // 2 < LAST_B]

        VECTOR_STEPS = ("clip", "embedding", "norm_a", "norm2", "norm_eps", "norm_inv", "unit", "recv",
                        "recv_diag", "same", "same_earlier", "repeated", "keep_first", "target", "dot",
                        "scalar_blocks", "vector_blocks", "dot_a", "unit_blocks", "dot_b", "dot_block", "sum")
        SCALAR_STEPS = ("square", "gauss_arg", "gauss", "norm", "hidden0", "hidden1", "weights", "placed")
        TENSOR_STEPS = ("lengths", "receivers", "hidden0", "hidden1", "weights", "placed", "update")
        TILE_LOADS = 4

        def tile_step(eng, signal, steps, i, name):
            eng.wait_ge(signal, i * len(steps) + steps.index(name) + 1)

        hidden_seq = 2 * (SUB // HCOL)
        assert hidden_seq == 8 and HALF_V * P == 4 * 512 - 256
        W_GROUPS = 4

        block = ctx.enter_context(nc.Block())

        @block.sync
        def _(sp):
            def load_rows(k, b, at):
                c = 2 * k + b
                b_tiles = LAST_B if at == CHUNKS - 1 else T
                if from_chunk(at, 2):
                    sp.wait_ge(edge_scalars, c - 1)
                    sp.wait_ge(left_ready, c - 1)
                    sp.wait_ge(transposed, c - 1)
                done = rows_loaded[b]
                for p0, t0, n in sub_rows(b_tiles):
                    first = c * V + t0
                    sp.dma_start(src_row[b][p0:p0 + n, :], src2[bass.ds(first, n), :]).then_inc(done, 16)
                    sp.dma_start(dst_row[b][p0:p0 + n, :], dst2[bass.ds(first, n), :]).then_inc(done, 16)
                    sp.dma_start(attr_row[b][p0:p0 + n, :, :].rearrange("t p c -> t (p c)"),
                                 attr2[bass.ds(first, n), :]).then_inc(done, 16)
                with nc.allow_non_contiguous_dma(reason="one receiver to every partition"):
                    for s in range(2):
                        sub0 = dst_flat[:, bass.ds(c * CHUNK + s * SUB, 1)]
                        sp.dma_start(base[b][s * WINDOW:(s + 1) * WINDOW, 0:1],
                                     sub0.broadcast_to([WINDOW, 1])).then_inc(done, 16)
                    sp.dma_start(base[b][:, 1:2], dst_flat[:, bass.ds(c * CHUNK, 1)].broadcast_to([P, 1]))\
                      .then_inc(done, 16)
                if at != CHUNKS - 1:
                    r = r_flat[bass.ds(c * CHUNK, CHUNK)].rearrange("(g j) -> g j", g=16)
                    sp.dma_start(r_in[b][0:16, :], r).then_inc(done, 16)
                else:
                    edges = EDGES - c * CHUNK
                    whole, rest = edges // GROUP, edges % GROUP
                    r = r_flat[c * CHUNK:c * CHUNK + whole * GROUP].rearrange("(g j) -> g j", g=whole)
                    sp.dma_start(r_in[b][0:whole, :], r).then_inc(done, 16)
                    r = r_flat[c * CHUNK + whole * GROUP:EDGES].rearrange("(a j) -> a j", a=1)
                    sp.dma_start(r_in[b][whole:whole + 1, 0:rest], r).then_inc(done, 16)

            def load_x(g, ring):
                r = x[bass.ds(g * NG * P, NG * P), :].rearrange("(t p) f -> p t f", p=P)
                sp.dma_start(x_ring[:, ring, :, :], r).then_inc(x_loaded[ring], 16)

            def const(dst_ap, src_ap):
                n_const[0] = n_const.get(0, 0) + 1
                sp.dma_start(dst_ap, src_ap).then_inc(const_loaded, 16)

            for g in range(RING):
                load_x(g, g)
            sp.wait_ge(const_step, 1)
            const(wup_raw[0:MUL, 0:MUL], W_up0)
            for c in range(3):
                const(wup_raw[MUL + c:MUL + c + 3 * (MUL - 1) + 1:3, MUL * (c + 1):MUL * (c + 2)], W_up1)
            load_rows(0, 0, 0)
            for g in range(16):
                const(w0_rep[g * CENTERS:(g + 1) * CENTERS, :], mlp_w0)
            for s in range(2):
                const(w1_diag[s * HID:(s + 1) * HID, s * HID:(s + 1) * HID], mlp_w1)
                const(w2_diag[s * HID:(s + 1) * HID, s * P:(s + 1) * P], mlp_w2)
                with nc.allow_non_contiguous_dma(reason="biases"):
                    const(bias01[s * HID:(s + 1) * HID, 0:1], mlp_b0.rearrange("(p a) -> p a", a=1))
                    const(bias01[s * HID:(s + 1) * HID, 1:2], mlp_b1.rearrange("(p a) -> p a", a=1))
            const(b2_rep[:, :], mlp_b2.rearrange("(a n) -> a n", a=1).broadcast_to([P, P]))
            const(wout_raw[0:HID, 0, :], W_out0)
            const(wout_raw[HID:P, 0, :], W_out1)
            const(wout_raw[0:HID, 1, :], W_out1)
            const(wout_raw[HID:P, 1, :], W_out1)
            load_rows(0, 1, 1)
            sp.dma_start(node_sum[NODES:NODES + P, :], zeros[:, :]).then_inc(pad_saved, 16)

            def save_group(g, ring, k, whole=True):
                sp.wait_ge(x_loaded[ring], 16 * (k + 1))
                if whole:
                    where = node_sum[bass.ds(g * NG * P, NG * P), :].rearrange("(t p) f -> p t f", p=P)
                    sp.dma_start(where, x_ring[:, ring, :, :]).then_inc(x_saved[ring], 16)
                    sp.wait_ge(proj_copied, g + 1)
                    where = table[bass.ds(g * NG * P, NG * P), :].rearrange("(t p) f -> p t f", p=P)
                    sp.dma_start(where, proj[:, ring % 2, :].rearrange("p (t f) -> p t f", f=P))\
                      .then_inc(proj_saved[ring % 2], 16)

            with sp.Fori(0, NODE_GROUPS // RING - 1) as k:
                for ring in range(RING):
                    save_group(RING * k + ring, ring, k)
                    sp.wait_ge(x_saved[ring], 16 * (k + 1))
                    sp.wait_ge(xT_ready, RING * k + ring + 1)
                    load_x(RING * (k + 1) + ring, ring)
            k = NODE_GROUPS // RING - 1
            for ring in range(RING):
                save_group(RING * k + ring, ring, k)
                if ring == 0:
                    sp.wait_ge(x_saved[0], 16 * (k + 1))
                    sp.wait_ge(xT_ready, RING * k + 1)
                    row = NODE_GROUPS * NG * P
                    sp.dma_start(x_ring[:, 0, 0, :], x[row:row + P, :]).then_inc(x_loaded[0], 16)
                    sp.dma_start(x_ring[0:LAST_NODES, 0, 1, :], x[row + P:NODES, :]).then_inc(x_loaded[0], 16)
            sp.wait_ge(x_loaded[0], 16 * (k + 1) + 32)
            row = NODE_GROUPS * NG * P
            sp.dma_start(node_sum[row:row + P, :], x_ring[:, 0, 0, :]).then_inc(x_saved[0], 16)
            sp.dma_start(node_sum[row + P:NODES, :], x_ring[0:LAST_NODES, 0, 1, :]).then_inc(x_saved[0], 16)
            sp.wait_ge(proj_copied, NODE_GROUPS + 1)
            sp.dma_start(table[row:row + P, :], proj[:, 0, 0:P]).then_inc(proj_saved[0], 16)
            sp.dma_start(table[row + P:NODES, :], proj[0:LAST_NODES, 0, P:2 * P]).then_inc(proj_saved[0], 16)

            sp.wait_ge(x_saved[0], 16 * (NODE_GROUPS // RING) + 32)
            for ring in range(1, RING):
                sp.wait_ge(x_saved[ring], 16 * (NODE_GROUPS // RING))
            sp.wait_ge(pad_saved, 16)

            def chunk(k, b, at):
                c = 2 * k + b
                b_tiles = LAST_B if at == CHUNKS - 1 else T
                if has_next(at, 2):
                    load_rows(k + 1, b, None if at is None else at + 2)
                sp.wait_ge(left_ready, c + 1)
                for p0, t0, n in sub_rows(b_tiles):
                    sp.dma_start(leftover[bass.ds(c * V + t0, n), :], left_row[b][p0:p0 + n, :])\
                      .then_inc(left_saved[b], 16)
                first_node = sp.value_load(dst_flat[0:1, bass.ds(c * CHUNK, 1)], min_val=0, max_val=NODES - 1)
                if from_chunk(at, 1):
                    sp.wait_ge(window_saved, 16 * c)
                window = node_sum[bass.ds(first_node, P), :]
                sp.dma_start(old_sum[:, :], window).then_inc(window_read, 16)
                sp.wait_ge(window_added, c + 1)
                sp.dma_start(window, new_sum[:, :]).then_inc(window_saved, 16)

            each_chunk(sp, chunk)

            sp.wait_ge(window_saved, 16 * CHUNKS)
            for b in range(2):
                sp.wait_ge(left_saved[b], 16 * CHUNKS)
            sp.wait_ge(flag_ready, 1)
            with sp.If(sp.value_load(flag[0:1, 0:1], min_val=0, max_val=P) > 0):
                with sp.Fori(0, EDGE_TILES) as i:
                    with nc.allow_non_contiguous_dma(reason="one edge to every partition"):
                        sp.dma_start(one_src[:, :], src2[bass.ds(i, 1), :].rearrange("a p -> p a"))\
                          .then_inc(tile_loaded, 16)
                        sp.dma_start(one_left[:, :], leftover[bass.ds(i, 1), :].rearrange("a p -> p a"))\
                          .then_inc(tile_loaded, 16)
                    sp.dma_start(one_attr[:, :], attr2[bass.ds(i, 1), :].rearrange("a (p c) -> (a p) c", c=3))\
                      .then_inc(tile_loaded, 16)
                    sp.dma_start(r_in[0][0:1, 0:P], r_flat[bass.ds(i * P, P)].rearrange("(a j) -> a j", a=1))\
                      .then_inc(tile_loaded, 16)
                    sp.wait_ge(tile_saved, 16 * i + 16)
                    sp.sem_inc(tile_done, 1)
            groups = NODE_TILES // LG
            for g in range(groups + 2):
                if g < groups:
                    if g >= 2:
                        sp.wait_ge(ln_ready, g - 1)
                    n = LG if g < groups - 1 else LG - 1
                    r0 = g * LG * P
                    sp.dma_start(ln_in[g % 2][:, 0:n, :],
                                 node_sum[r0:r0 + n * P, :].rearrange("(t p) f -> p t f", p=P))\
                      .then_inc(norm_loaded[g % 2], 16)
                    if n < LG:
                        sp.dma_start(ln_in[g % 2][:, n, :], node_sum[r0 + n * P:r0 + LG * P, :])\
                          .then_inc(norm_loaded[g % 2], 16)
                if 1 <= g <= groups:
                    o = g - 1
                    sp.wait_ge(ln_ready, o + 1)
                    n = LG if o < groups - 1 else LG - 1
                    r0 = o * LG * P
                    sp.dma_start(out[r0:r0 + n * P, :].rearrange("(t p) f -> p t f", p=P),
                                 ln_out[o % 2][:, 0:n, :]).then_inc(out_saved[o % 2], 16)
                    if n < LG:
                        sp.dma_start(out[r0 + n * P:NODES, :], ln_out[o % 2][0:LAST_NODES, n, :])\
                          .then_inc(out_saved[o % 2], 16)
            assert groups % 2 == 1
            sp.wait_ge(out_saved[0], 16 * (groups // 2 + 2))
            sp.wait_ge(out_saved[1], 16 * (groups // 2))

        @block.gpsimd
        def _(pool):
            def step(ins):
                ins.then_inc(const_pool, 1)
                n_const[1] = n_const.get(1, 0) + 1
                return n_const[1]

            step(nc.gpsimd.iota(iota_i[:, :], pattern=[[1, P]], base=0, channel_multiplier=0))
            step(nc.gpsimd.iota(pcol_i[:, 0:1], pattern=[[1, 1]], base=0, channel_multiplier=1))
            step(nc.gpsimd.memset(ident[:, :], 0.0))
            step(nc.gpsimd.memset(group_low[:, :], 1.0))
            n = step(nc.gpsimd.memset(row_select[:, :], 0.0))
            pool.wait_ge(const_pool, n)
            step(nc.gpsimd.affine_select(out=ident[:, :], in_=ident[:, :], compare_op=ALU.not_equal, fill=1.0,
                                         base=0, pattern=[[-1, P]], channel_multiplier=1))
            sel = row_select[:, :].rearrange("p (t s) -> p t s", s=2)
            step(nc.gpsimd.affine_select(out=sel, in_=sel, compare_op=ALU.not_equal, fill=1.0, base=0,
                                         pattern=[[-1, T], [-WINDOW, 2]], channel_multiplier=1))
            pool.wait_ge(const_step, 1)
            n = step(nc.gpsimd.affine_select(out=group_low[:, :], in_=group_low[:, :], compare_op=ALU.is_ge,
                                             fill=0.0, base=0, pattern=[[1, P]], channel_multiplier=-CENTERS))
            pool.wait_ge(const_pool, n)
            step(nc.gpsimd.affine_select(out=group_rep[:, :], in_=group_low[:, :], compare_op=ALU.is_ge,
                                         fill=0.0, base=CENTERS - 1, pattern=[[-1, P]],
                                         channel_multiplier=CENTERS))
            step(nc.gpsimd.affine_select(out=earlier[:, :], in_=ones[:, :], compare_op=ALU.is_gt, fill=0.0,
                                         base=0, pattern=[[-1, P]], channel_multiplier=1))
            pool.wait_ge(const_step, W0_WIDE)
            pattern = [[-CENTERS, 8], [-HID, 2], [0, HID]]
            n = step(nc.gpsimd.affine_select(out=w0_keep[:, :, :, :], in_=w0_wide[:, :, :, :],
                                             compare_op=ALU.is_ge, fill=0.0, base=0, pattern=pattern,
                                             channel_multiplier=1))
            pool.wait_ge(const_pool, n)
            pattern = [[CENTERS, 8], [HID, 2], [0, HID]]
            step(nc.gpsimd.affine_select(out=w0_groups[:, :, :, :], in_=w0_keep[:, :, :, :],
                                         compare_op=ALU.is_ge, fill=0.0, base=CENTERS - 1, pattern=pattern,
                                         channel_multiplier=-1))

            pool.wait_ge(proj_saved[0], 16 * (NODE_GROUPS // 2) + 32)
            pool.wait_ge(proj_saved[1], 16 * (NODE_GROUPS // 2))

            def chunk(k, b, at):
                c = 2 * k + b
                pool.wait_ge(idx_ready, c + 1)
                for h in range(2):
                    if from_chunk(at, 2):
                        pool.wait_ge(msg_ready, 2 * (c - 2) + h + 1)
                        pool.sem_inc(rows_free, 1)
                    for v in last_tiles(at, h):
                        pool.indirect_dma_start(rows[b][h][:, v - h * HALF_V, :], None, table[:, :],
                                                bass.IndirectOffsetOnAxis(ap=idx[b][:, v:v + 1], axis=0))\
                            .then_inc(gathered[b][h], 16)

            each_chunk(pool, chunk)

            pool.wait_ge(flag_ready, 1)
            with pool.If(pool.value_load(flag[0:1, 0:1], min_val=0, max_val=P) > 0):
                with pool.Fori(0, EDGE_TILES) as i:
                    pool.wait_ge(tile_loaded, 16 * TILE_LOADS * i + 16 * TILE_LOADS)
                    pool.sem_inc(rows_free, 1)
                    pool.indirect_dma_start(rows[0][0][:, 0, :], None, table[:, :],
                                            bass.IndirectOffsetOnAxis(ap=one_src[:, :], axis=0))\
                        .then_inc(tile_rows, 16)
                    pool.indirect_dma_start(old_sum[:, :], None, node_sum[:, :],
                                            bass.IndirectOffsetOnAxis(ap=one_left[:, :], axis=0))\
                        .then_inc(tile_sums, 16)
                    tile_step(pool, tile_vector, VECTOR_STEPS, i, "sum")
                    pool.sem_inc(rows_free, 1)
                    pool.indirect_dma_start(node_sum[:, :], bass.IndirectOffsetOnAxis(ap=target[:, :], axis=0),
                                            new_sum[:, :], None).then_inc(tile_saved, 16)

        @block.tensor
        def _(pe):
            pe.wait_ge(const_pool, 6)
            pe.wait_ge(const_step, WUP)

            def transpose_nodes(g, ring, k, tiles, wait):
                pe.wait_ge(x_loaded[ring], wait)
                if tiles:
                    for i, n in enumerate(tiles):
                        last = nc.tensor.matmul(hid_ps[ring % 2][:, i * P:i * P + n], x_ring[0:n, ring, i, :],
                                                ident[0:n, 0:n], start=True, stop=True)
                    last.then_inc(xT_ready, 1)

            def project_nodes(g, half, tiles):
                pe.wait_ge(xT_copied, g + 1)
                for i, n in enumerate(tiles):
                    last = nc.tensor.matmul(w_ps[half][0:n, i * P:(i + 1) * P], xT[:, half, i * P:i * P + n],
                                            wup[:, :], start=True, stop=True)
                last.then_inc(proj_ready, 1)

            whole = [P] * NG
            short = [P] * (SHORT - 1) + [LAST_NODES]
            def node_group(g, ring, k, first=False):
                if not first:
                    pe.wait_ge(xT_copied, g - 1)
                transpose_nodes(g, ring, k, whole, 16 * (k + 1))

            for ring in range(RING):
                node_group(ring, ring, 0, first=ring < 2)
                if ring >= 1:
                    if ring >= 3:
                        pe.wait_ge(proj_copied, ring - 2)
                    project_nodes(ring - 1, (ring - 1) % 2, whole)
            with pe.Fori(1, NODE_GROUPS // RING) as k:
                for ring in range(RING):
                    g = RING * k + ring
                    node_group(g, ring, k)
                    pe.wait_ge(proj_copied, g - 2)
                    project_nodes(g - 1, (ring - 1) % 2, whole)
            pe.wait_ge(xT_copied, NODE_GROUPS - 1)
            transpose_nodes(NODE_GROUPS, 0, 0, short, 16 * (NODE_GROUPS // RING) + 32)
            pe.wait_ge(proj_copied, NODE_GROUPS - 2)
            project_nodes(NODE_GROUPS - 1, 1, whole)
            pe.wait_ge(proj_copied, NODE_GROUPS - 1)
            project_nodes(NODE_GROUPS, 0, short)
            pe.wait_ge(xT_copied, NODE_GROUPS + 1)
            pe.wait_ge(proj_copied, NODE_GROUPS + 1)
            pe.wait_ge(const_step, CONST_STEPS)
            pe.wait_ge(const_pool, 12)

            def transpose_rows(k, b, at):
                c = 2 * k + b
                pe.wait_ge(rows_ready, c + 1)
                pe.wait_ge(rows_loaded[b], loaded_count(k, at))
                if from_chunk(at, 1):
                    pe.wait_ge(unit_ready, c)
                    pe.wait_ge(one_hot_ready, c)
                    pe.wait_ge(emb_ready, c)
                for i, lhs in enumerate([src_f[:, :], rel[:, :]] + [attr_row[b][:, :, j] for j in range(3)]):
                    last = nc.tensor.matmul(row_ps[:, i * V:(i + 1) * V], lhs, row_select[:, :],
                                            start=True, stop=True)
                last = nc.tensor.matmul(row_ps[:, 5 * V:5 * V + GROUP], group_rep[:, :], r_in[b][:, :],
                                        start=True, stop=True)
                last.then_inc(transposed, 1)

            def hidden(k, b, at, layer):
                c = 2 * k + b
                if layer == 0:
                    pe.wait_ge(emb_ready, c + 1)
                for i in range(4):
                    n = 4 * layer + i
                    if from_chunk(at, 1) or n >= 2:
                        pe.wait_ge(hid_copied, 8 * c + n - 1)
                    bank = hid_ps[n % 2]
                    if layer == 0:
                        for j in range(2):
                            q = 2 * i + j
                            last = nc.tensor.matmul(bank[:, j * GROUP:(j + 1) * GROUP],
                                                    w0_groups[:, q, :, :].rearrange("p s f -> p (s f)"),
                                                    emb[:, :], start=True, stop=True)
                    else:
                        last = nc.tensor.matmul(bank[:, 0:HCOL], w1_diag[:, :], h1[:, i * HCOL:(i + 1) * HCOL],
                                                start=True, stop=True)
                    last.then_inc(hid_ready, 1)

            def edge_weights(k, b, at, h):
                c = 2 * k + b
                pe.wait_ge(hid_copied, 8 * c + 8)
                for i in range(W_GROUPS):
                    m = h * W_GROUPS + i
                    if from_chunk(at, 1) or m >= 2:
                        pe.wait_ge(w_copied, 8 * c + m - 1)
                    bank = w_ps[m % 2]
                    pairs = range(7 * h + 2 * i, min(7 * h + 2 * i + 2, 7 * h + 7))
                    width = 2 * P * len(pairs)
                    nc.tensor.matmul(bank[:, 0:width], ones_bf[:, :],
                                     b2_rows[:, 0:2 * len(pairs), :].rearrange("p a f -> p (a f)"),
                                     start=True, stop=False)
                    for j, t in enumerate(pairs):
                        last = nc.tensor.matmul(bank[:, 2 * P * j:2 * P * (j + 1)], h2[b][:, t * P:(t + 1) * P],
                                                w2_diag[:, :], start=False, stop=j == len(pairs) - 1)
                    last.then_inc(w_ready, 1)

            def sum_messages(k, b, at, h):
                c = 2 * k + b
                pe.wait_ge(msg_ready, 2 * c + h + 1)
                if h == 0:
                    pe.wait_ge(one_hot_ready, c + 1)
                    if from_chunk(at, 1):
                        pe.wait_ge(win_copied, c)
                ends = [max(v for v in last_tiles(at, 0) + last_tiles(at, 1) if v % 2 == s) for s in range(2)]
                for v in last_tiles(at, h):
                    s = v % 2
                    last = nc.tensor.matmul(win_ps[s * WINDOW:(s + 1) * WINDOW, 0:MSG], one_hot[b][:, v, :],
                                            msg[h][:, v - h * HALF_V, 0:MSG], start=v < 2, stop=v == ends[s])
                last.then_inc(msg_summed, 1)

            def place_windows(k, b):
                c = 2 * k + b
                pe.wait_ge(win_copied, c + 1)
                pe.wait_ge(place_ready, c + 1)
                for j in range(2):
                    last = nc.tensor.matmul(upd_ps[:, j * P:(j + 1) * P], win_sb[:, j * P:(j + 1) * P],
                                            place[b][:, :], start=True, stop=True)
                last.then_inc(placed, 1)

            def project_out(k, b, at):
                c = 2 * k + b
                pe.wait_ge(placed_copied, c + 1)
                if from_chunk(at, 1):
                    pe.wait_ge(window_added, c)
                for j in range(2):
                    last = nc.tensor.matmul(upd_ps[:, 2 * P:3 * P], nodesT[:, j * P:(j + 1) * P],
                                            wout[:, j, :], start=j == 0, stop=j == 1)
                last.then_inc(upd_ready, 1)

            def back(k, b):
                return (k, 0) if b else (k - 1, 1)

            def chunk(k, b, at):
                nxt = after(k, b)
                at_next = None if at is None else at + 1
                if has_next(at):
                    transpose_rows(*nxt, at_next)
                edge_weights(k, b, at, 1)
                if from_chunk(at, 1):
                    place_windows(*back(k, b))
                if has_next(at):
                    hidden(*nxt, at_next, 0)
                if from_chunk(at, 1):
                    project_out(*back(k, b), None if at is None else at - 1)
                if has_next(at):
                    hidden(*nxt, at_next, 1)
                sum_messages(k, b, at, 0)
                if has_next(at):
                    edge_weights(*nxt, at_next, 0)
                sum_messages(k, b, at, 1)

            transpose_rows(0, 0, 0)
            hidden(0, 0, 0, 0)
            hidden(0, 0, 0, 1)
            edge_weights(0, 0, 0, 0)
            each_chunk(pe, chunk)
            k, b = (CHUNKS - 1) // 2, (CHUNKS - 1) % 2
            place_windows(k, b)
            project_out(k, b, CHUNKS - 1)

            pe.wait_ge(flag_step, 3)
            nc.tensor.matmul(row_ps[0:1, 0:1], valid_row[:, :], missed_col[:, 1:2], start=True, stop=True)\
              .then_inc(flag_summed, 1)
            pe.wait_ge(flag_ready, 1)
            with pe.If(pe.value_load(flag[0:1, 0:1], min_val=0, max_val=P) > 0):
                with pe.Fori(0, EDGE_TILES) as i:
                    pe.wait_ge(tile_loaded, 16 * TILE_LOADS * i + 16 * TILE_LOADS)
                    nc.tensor.matmul(row_ps[:, 0:P], group_rep[:, :], r_in[0][:, 0:P], start=True, stop=True)\
                      .then_inc(tile_tensor, 1)
                    tile_step(pe, tile_vector, VECTOR_STEPS, i, "recv_diag")
                    nc.tensor.matmul(row_ps[:, P:2 * P], ones[:, :], recv_diag[:, :], start=True, stop=True)\
                      .then_inc(tile_tensor, 1)
                    tile_step(pe, tile_vector, VECTOR_STEPS, i, "embedding")
                    nc.tensor.matmul(hid_ps[0][:, 0:P], w0_groups[:, 0, :, :].rearrange("p s f -> p (s f)"),
                                     emb[:, 0:P], start=True, stop=True).then_inc(tile_tensor, 1)
                    tile_step(pe, tile_scalar, SCALAR_STEPS, i, "hidden0")
                    nc.tensor.matmul(hid_ps[1][:, 0:P], w1_diag[:, :], h1[:, 0:P], start=True, stop=True)\
                      .then_inc(tile_tensor, 1)
                    tile_step(pe, tile_scalar, SCALAR_STEPS, i, "hidden1")
                    nc.tensor.matmul(w_ps[0][:, 0:P], ones_bf[:, :], b2_rows[:, 0, :], start=True, stop=False)
                    nc.tensor.matmul(w_ps[0][:, 0:P], h2[0][:, 0:P], w2_diag[:, 0:P], start=False, stop=True)\
                      .then_inc(tile_tensor, 1)
                    tile_step(pe, tile_vector, VECTOR_STEPS, i, "dot_block")
                    for j in range(2):
                        last = nc.tensor.matmul(upd_ps[:, j * P:(j + 1) * P], msg[0][:, 0, j * P:(j + 1) * P],
                                                same[:, :], start=True, stop=True)
                    last.then_inc(tile_tensor, 1)
                    tile_step(pe, tile_scalar, SCALAR_STEPS, i, "placed")
                    for j in range(2):
                        last = nc.tensor.matmul(upd_ps[:, 2 * P:3 * P], nodesT[:, j * P:(j + 1) * P],
                                                wout[:, j, :], start=j == 0, stop=j == 1)
                    last.then_inc(tile_tensor, 1)

        @block.scalar
        def _(act):
            def node_group(g, ring, first=False):
                act.wait_ge(xT_ready, g + 1)
                if not first:
                    act.wait_ge(proj_ready, g - 1)
                nc.scalar.activation(xT[:, ring % 2, :], hid_ps[ring % 2][:, :], ACT.Copy).then_inc(xT_copied, 1)

            for ring in range(RING):
                node_group(ring, ring, first=ring < 2)
            with act.Fori(1, NODE_GROUPS // RING) as k:
                for ring in range(RING):
                    node_group(RING * k + ring, ring)
            act.wait_ge(xT_ready, NODE_GROUPS + 1)
            act.wait_ge(proj_ready, NODE_GROUPS - 1)
            n = (SHORT - 1) * P + LAST_NODES
            nc.scalar.activation(xT[:, 0, 0:n], hid_ps[0][:, 0:n], ACT.Copy).then_inc(xT_copied, 1)
            act.wait_ge(const_step, CONST_STEPS)

            def copy_windows(c):
                act.wait_ge(msg_summed, 2 * (c + 1))
                nc.scalar.activation(win_sb[:, :], win_ps[:, 0:MSG], ACT.Copy).then_inc(win_copied, 1)

            def gaussians(c):
                act.wait_ge(clip_ready, c + 1)
                nc.scalar.activation(gauss_arg[:, :], r_clip[:, :], ACT.Square, bias=minus_center[:, 0:1],
                                     scale=float(CENTERS - 1)).then_inc(gauss_step, 1)
                act.wait_ge(gauss_step, 2 * c + 1)
                nc.scalar.activation(gauss[:, :], gauss_arg[:, :], ACT.Exp, scale=-0.5).then_inc(gauss_step, 1)

            def norms(c):
                act.wait_ge(transposed, c + 1)
                nc.scalar.activation(square[:, :, :], row_ps[:, 2 * V:5 * V].rearrange("p (c v) -> p c v", c=3),
                                     ACT.Square).then_inc(squared, 1)
                act.wait_ge(norm2_ready, c + 1)
                nc.scalar.activation(norm[:, :], norm2[:, :], ACT.Sqrt).then_inc(norm_ready, 1)

            def silus(c, b):
                for n in range(8):
                    act.wait_ge(hid_ready, 8 * c + n + 1)
                    layer, i = divmod(n, 4)
                    to = h1 if layer == 0 else h2[b]
                    nc.scalar.activation(to[:, i * HCOL:(i + 1) * HCOL], hid_ps[n % 2][:, 0:HCOL], ACT.Silu,
                                         bias=bias01[:, layer:layer + 1]).then_inc(hid_copied, 1)

            def copy_weights(k, b, at, h):
                c = 2 * k + b
                if from_chunk(at, 1):
                    act.wait_ge(msg_ready, 2 * (c - 1) + h + 1)
                for i in range(W_GROUPS):
                    m = h * W_GROUPS + i
                    n = min(4, HALF_V - 4 * i)
                    act.wait_ge(w_ready, 8 * c + m + 1)
                    nc.scalar.activation(w_edge[h][:, 4 * i:4 * i + n, :],
                                         w_ps[m % 2][:, 0:n * P].rearrange("p (v f) -> p v f", f=P),
                                         ACT.Copy).then_inc(w_copied, 1)

            def copy_placed(c):
                act.wait_ge(placed, c + 1)
                nc.scalar.activation(nodesT[:, :], upd_ps[:, 0:MSG], ACT.Copy).then_inc(placed_copied, 1)

            def chunk(k, b, at):
                c = 2 * k + b
                nxt = after(k, b)
                at_next = None if at is None else at + 1
                if from_chunk(at, 1):
                    copy_windows(c - 1)
                if has_next(at):
                    gaussians(c + 1)
                    norms(c + 1)
                copy_weights(k, b, at, 1)
                if from_chunk(at, 1):
                    copy_placed(c - 1)
                if has_next(at):
                    silus(c + 1, nxt[1])
                    copy_weights(*nxt, at_next, 0)

            gaussians(0)
            norms(0)
            silus(0, 0)
            copy_weights(0, 0, 0, 0)
            each_chunk(act, chunk)
            copy_windows(CHUNKS - 1)
            copy_placed(CHUNKS - 1)

            act.wait_ge(flag_ready, 1)
            with act.If(act.value_load(flag[0:1, 0:1], min_val=0, max_val=P) > 0):
                with act.Fori(0, EDGE_TILES) as i:
                    act.wait_ge(tile_loaded, 16 * TILE_LOADS * i + 16 * TILE_LOADS)
                    nc.scalar.activation(one_square[:, :], one_attr[:, :], ACT.Square).then_inc(tile_scalar, 1)
                    tile_step(act, tile_vector, VECTOR_STEPS, i, "clip")
                    nc.scalar.activation(gauss_arg[:, 0:P], r_clip[:, 0:P], ACT.Square, bias=minus_center[:, 0:1],
                                         scale=float(CENTERS - 1)).then_inc(tile_scalar, 1)
                    tile_step(act, tile_scalar, SCALAR_STEPS, i, "gauss_arg")
                    nc.scalar.activation(gauss[:, 0:P], gauss_arg[:, 0:P], ACT.Exp, scale=-0.5)\
                      .then_inc(tile_scalar, 1)
                    tile_step(act, tile_vector, VECTOR_STEPS, i, "norm2")
                    nc.scalar.activation(one_norm[:, 2:3], one_norm[:, 1:2], ACT.Sqrt).then_inc(tile_scalar, 1)
                    for layer, (name, to) in enumerate((("hidden0", h1), ("hidden1", h2[0]))):
                        tile_step(act, tile_tensor, TENSOR_STEPS, i, name)
                        nc.scalar.activation(to[:, 0:P], hid_ps[layer][:, 0:P], ACT.Silu,
                                             bias=bias01[:, layer:layer + 1]).then_inc(tile_scalar, 1)
                    tile_step(act, tile_tensor, TENSOR_STEPS, i, "weights")
                    nc.scalar.activation(w_edge[0][:, 0, :], w_ps[0][:, 0:P], ACT.Copy).then_inc(tile_scalar, 1)
                    tile_step(act, tile_tensor, TENSOR_STEPS, i, "placed")
                    nc.scalar.activation(nodesT[:, :], upd_ps[:, 0:MSG], ACT.Copy).then_inc(tile_scalar, 1)

            for g in range(NODE_TILES // LG):
                act.wait_ge(ln_var, g + 1)
                nc.scalar.activation(ln_sd[:, :], ln_eps[:, :], ACT.Sqrt).then_inc(ln_std, 1)

        @block.vector
        def _(dve):
            n_dve = [0]

            def step(ins):
                ins.then_inc(const_step, 1)
                n_dve[0] += 1
                return n_dve[0]

            def settle():
                dve.wait_ge(const_step, n_dve[0])

            for tile in (wup_raw[:, :], w1_diag[:, :], w2_diag[:, :], wout[:, :, :], zeros[:, :],
                         src_row[0][:, :], src_row[1][:, :], dst_row[0][:, :], dst_row[1][:, :]):
                nc.vector.memset(tile, 0)
            for b in range(2):
                nc.vector.memset(attr_row[b][:, :, :], 0.0)
                nc.vector.memset(r_in[b][:, :], 0.0)
            nc.vector.memset(ones[:, :], 1.0)
            step(nc.vector.memset(missed_any[:, :], 0.0))
            nc.vector.memset(ones_bf[:, :], 1.0)
            nc.vector.memset(wout_scale[:, :], 1.0 / 128)
            dve.wait_ge(const_pool, 2)
            step(nc.vector.tensor_copy(iota_f[:, :], iota_i[:, :]))
            step(nc.vector.tensor_copy(pcol[:, :], pcol_i[:, 0:1]))
            step(nc.vector.tensor_single_scalar(pcol_i[:, 1:2], pcol_i[:, 0:1], WINDOW - 1, op=ALU.bitwise_and))
            step(nc.vector.tensor_single_scalar(pcol_i[:, 2:3], pcol_i[:, 0:1], CENTERS - 1, op=ALU.bitwise_and))
            settle()
            for half, p0 in ((0, 64), (1, 0), (1, 64)):
                nc.vector.memset(wout_scale[p0:p0 + MUL, half:half + 1], math.sqrt(3.0) / 128)
            step(nc.vector.tensor_scalar(trash_row[:, :], iota_f[:, :], float(NODES), None, ALU.add))
            step(nc.vector.tensor_copy(window_lane[:, :], pcol_i[:, 1:2]))
            step(nc.vector.tensor_scalar(minus_center[:, :], pcol_i[:, 2:3], -1.0, None, ALU.mult))
            dve.wait_ge(const_loaded, 16 * CONST_DMAS)
            assert step(nc.vector.tensor_scalar(wup[:, :], wup_raw[:, :], 1.0 / math.sqrt(MUL), None, ALU.mult)) == WUP
            assert step(nc.vector.tensor_scalar(
                w0_wide[:, :, :, :].rearrange("p q s f -> p (q s) f"), spread(w0_rep[:, :], 1, 16),
                math.sqrt(CENTERS), None, ALU.mult)) == W0_WIDE
            step(nc.vector.tensor_copy(b2_part[:, 0, :], b2_rep[:, :]))
            settle()
            step(nc.vector.tensor_tensor(b2_rest[:, 0, :], b2_rep[:, :], b2_part[:, 0, :], ALU.subtract))
            settle()
            step(nc.vector.tensor_copy(b2_part[:, 1, :], b2_rest[:, 0, :]))
            settle()
            step(nc.vector.tensor_tensor(b2_rest[:, 1, :], b2_rest[:, 0, :], b2_part[:, 1, :], ALU.subtract))
            for i in range(3):
                step(nc.vector.tensor_scalar(b2_mask[:, i:i + 1], pcol[:, :], float(i), None, ALU.is_equal))
            settle()
            step(nc.vector.tensor_copy(b2_part[:, 2, :], b2_rest[:, 1, :]))
            step(nc.vector.tensor_scalar(b2_sum[:, 0, :], b2_part[:, 0, :], b2_mask[:, 0:1], None, ALU.mult))
            settle()
            step(nc.vector.scalar_tensor_tensor(b2_sum[:, 1, :], b2_part[:, 1, :], b2_mask[:, 1:2],
                                                b2_sum[:, 0, :], ALU.mult, ALU.add))
            settle()
            step(nc.vector.scalar_tensor_tensor(b2_rows[:, :, :], spread(b2_part[:, 2, :], 1, 4), b2_mask[:, 2:3],
                                                spread(b2_sum[:, 1, :], 1, 4), ALU.mult, ALU.add))
            step(nc.vector.tensor_scalar(wout[0:HID, 0, 0:MUL], wout_raw[0:HID, 0, :], wout_scale[0:HID, 0:1],
                                         None, ALU.mult))
            for half, p0, c in ((0, HID, 0), (1, 0, 1), (1, HID, 2)):
                step(nc.vector.tensor_scalar(wout[p0:p0 + HID, half, MUL + c:MUL + c + 3 * (MUL - 1) + 1:3],
                                             wout_raw[p0:p0 + HID, half, :], wout_scale[p0:p0 + HID, half:half + 1],
                                             None, ALU.mult))
            assert n_dve[0] == CONST_STEPS, n_dve[0]
            settle()

            def node_group(g, ring, k, first=False):
                dve.wait_ge(proj_ready, g + 1)
                if not first:
                    dve.wait_ge(proj_saved[ring % 2], 16 * (2 * k + ring // 2))
                nc.vector.tensor_copy(proj[:, ring % 2, :], w_ps[ring % 2][:, :]).then_inc(proj_copied, 1)

            for ring in range(RING):
                node_group(ring, ring, 0, first=ring < 2)
            with dve.Fori(1, NODE_GROUPS // RING) as k:
                for ring in range(RING):
                    node_group(RING * k + ring, ring, k)
            dve.wait_ge(proj_ready, NODE_GROUPS + 1)
            dve.wait_ge(proj_saved[0], 16 * (NODE_GROUPS // 2))
            nc.vector.tensor_copy(proj[:, 0, 0:P], w_ps[0][:, 0:P])
            nc.vector.tensor_copy(proj[0:LAST_NODES, 0, P:2 * P], w_ps[0][0:LAST_NODES, P:2 * P])\
              .then_inc(proj_copied, 1)

            def edge_rows(k, b, at):
                c = 2 * k + b
                dve.wait_ge(rows_loaded[b], loaded_count(k, at))
                if from_chunk(at, 1):
                    dve.wait_ge(transposed, c)
                nc.vector.tensor_copy(src_f[:, :], src_row[b][:, :])
                nc.vector.tensor_scalar(rel[:, :], dst_row[b][:, :], base[b][:, 0:1], None, ALU.subtract)\
                  .then_inc(rows_ready, 1)
                nc.vector.scalar_tensor_tensor(window_node[b][:, :], base[b][:, 0:1], window_lane[:, 0:1],
                                               base[b][:, 1:2], ALU.add, ALU.subtract).then_inc(edge_scalars, 1)

            def leftovers(k, b, at):
                c = 2 * k + b
                nc.vector.tensor_scalar(chunk_rel[:, :], dst_row[b][:, :], base[b][:, 1:2], None, ALU.subtract)\
                  .then_inc(left_step, 1)
                nc.vector.tensor_tensor(above_trash[:, :], dst_row[b][:, :], trash_row[:, :], ALU.subtract)\
                  .then_inc(left_step, 1)
                dve.wait_ge(rows_ready, c + 1)
                nc.vector.scalar_tensor_tensor(window_out[:, :], rel[:, :], float(1 - WINDOW), rel[:, :],
                                               ALU.add, ALU.mult).then_inc(left_step, 1)
                dve.wait_ge(left_step, 7 * c + 1)
                nc.vector.scalar_tensor_tensor(chunk_out[:, :], chunk_rel[:, :], float(1 - P), chunk_rel[:, :],
                                               ALU.add, ALU.mult).then_inc(left_step, 1)
                dve.wait_ge(left_step, 7 * c + 4)
                nc.vector.tensor_tensor(missed[:, :], window_out[:, :], chunk_out[:, :], ALU.max)\
                  .then_inc(left_step, 1)
                dve.wait_ge(left_step, 7 * c + 5)
                nc.vector.scalar_tensor_tensor(missed_row[:, :], missed[:, :], 0.0, above_trash[:, :],
                                               ALU.is_gt, ALU.mult).then_inc(left_step, 1)
                full = at != CHUNKS - 1
                for p0, n in ((0, P),) if full else ((0, T), (WINDOW, LAST_B)):
                    last = nc.vector.tensor_tensor(missed_any[p0:p0 + n, :], missed_any[p0:p0 + n, :],
                                                   missed[p0:p0 + n, :], ALU.max)
                last.then_inc(left_step, 1)
                dve.wait_ge(left_step, 7 * c + 7)
                if from_chunk(at, 2):
                    dve.wait_ge(left_saved[b], 32 * k)
                nc.vector.tensor_tensor(left_row[b][:, :], missed_row[:, :], trash_row[:, :], ALU.add)\
                  .then_inc(left_ready, 1)

            def edge_columns(k, b, at):
                c = 2 * k + b
                dve.wait_ge(transposed, c + 1)
                if from_chunk(at, 2):
                    dve.wait_ge(gathered[b][1], 16 * HALF_V * k)
                nc.vector.tensor_copy(idx[b][:, :], row_ps[:, 0:V]).then_inc(idx_ready, 1)
                nc.vector.tensor_scalar(r_clip[:, :], row_ps[:, 5 * V:5 * V + GROUP], 0.0, 1.0, ALU.max, ALU.min)\
                  .then_inc(clip_ready, 1)
                dve.wait_ge(squared, c + 1)
                nc.vector.tensor_tensor(norm_a[:, :], square[:, 0, :], square[:, 1, :], ALU.add).then_inc(norm_step, 1)
                dve.wait_ge(norm_step, 3 * c + 1)
                nc.vector.tensor_tensor(norm2[:, :], norm_a[:, :], square[:, 2, :], ALU.add).then_inc(norm2_ready, 1)
                if from_chunk(at, 2):
                    dve.wait_ge(msg_summed, 2 * (c - 1))
                nc.vector.tensor_tensor(one_hot[b][:, :, :], spread(iota_f[:, 0:WINDOW], 1, V),
                                        spread(row_ps[:, V:2 * V], 2, WINDOW), ALU.is_equal)\
                  .then_inc(one_hot_ready, 1)
                dve.wait_ge(norm_ready, c + 1)
                nc.vector.tensor_scalar(norm_eps[:, :], norm[:, :], 1e-12, None, ALU.add).then_inc(norm_step, 1)
                dve.wait_ge(gauss_step, 2 * c + 2)
                if from_chunk(at, 1):
                    dve.wait_ge(hid_ready, 8 * c - 4)
                nc.vector.scalar_tensor_tensor(emb[:, :], row_ps[:, 5 * V:5 * V + GROUP], 1.0, gauss[:, :], ALU.is_le, ALU.mult)\
                  .then_inc(emb_ready, 1)
                dve.wait_ge(norm_step, 3 * c + 2)
                nc.vector.reciprocal(norm_inv[:, :], norm_eps[:, :]).then_inc(norm_step, 1)
                dve.wait_ge(norm_step, 3 * c + 3)
                nc.vector.tensor_tensor(unit[b][:, :, :], row_ps[:, 2 * V:5 * V].rearrange("p (c v) -> p c v", c=3),
                                        spread(norm_inv[:, :], 1, 3), ALU.mult).then_inc(unit_ready, 1)

            def window_place(k, b, at):
                c = 2 * k + b
                if from_chunk(at, 2):
                    dve.wait_ge(placed, c - 1)
                dve.wait_ge(edge_scalars, c + 1)
                nc.vector.tensor_scalar(place[b][:, :], iota_f[:, :], window_node[b][:, 0:1], None, ALU.is_equal)\
                  .then_inc(place_ready, 1)

            def messages(k, b, at, h):
                c = 2 * k + b
                n = 2 * c + h
                x_in, w, m = rows[b][h], w_edge[h], msg[h]
                count = 16 * HALF_V * k + 16 * len(last_tiles(at, h))
                dve.wait_ge(gathered[b][h], count)
                dve.wait_ge(unit_ready, c + 1)
                dve.wait_ge(w_copied, 4 * n + 4)
                m_blocks = m[:, :, :].rearrange("p v (k f) -> p v k f", f=MUL)
                w_blocks = w[:, :, :].rearrange("p v (k f) -> p v k f", f=MUL)
                xs = x_in[:, :, 0:MUL]
                xv = x_in[:, :, MUL:FEAT].rearrange("p v (c f) -> p v c f", f=MUL)
                y = unit[b][:, :, h * HALF_V:(h + 1) * HALF_V].rearrange("p c v -> p v c")
                nc.vector.tensor_tensor(dot[:, :, :, :], xv, spread(y, 3, MUL), ALU.mult).then_inc(msg_step, 1)
                if from_chunk(at, 1):
                    dve.wait_ge(msg_summed, n - 1)
                nc.vector.tensor_tensor(m_blocks[:, :, 0:9:8, :], w_blocks[:, :, 0:2, :], spread(xs, 2, 2), ALU.mult)\
                  .then_inc(msg_step, 1)
                nc.vector.tensor_tensor(m_blocks[:, :, 3:8:2, :], spread(w_blocks[:, :, 2, :], 2, 3), xv, ALU.mult)\
                  .then_inc(msg_step, 1)
                dve.wait_ge(msg_step, 5 * n + 2)
                nc.vector.tensor_tensor(dot_a[:, :, :], dot[:, :, 0, :], dot[:, :, 1, :], ALU.add).then_inc(msg_step, 1)
                nc.vector.tensor_tensor(m_blocks[:, :, 2:7:2, :], spread(m_blocks[:, :, 8, :], 2, 3),
                                        spread(y, 3, MUL), ALU.mult)
                dve.wait_ge(msg_step, 5 * n + 4)
                nc.vector.tensor_tensor(dot_b[:, :, :], dot_a[:, :, :], dot[:, :, 2, :], ALU.add).then_inc(msg_step, 1)
                dve.wait_ge(msg_step, 5 * n + 5)
                nc.vector.tensor_tensor(m_blocks[:, :, 1, :], dot_b[:, :, :], w_blocks[:, :, 3, :], ALU.mult)\
                  .then_inc(msg_ready, 1)

            def add_window(c):
                dve.wait_ge(upd_ready, c + 1)
                dve.wait_ge(window_read, 16 * (c + 1))
                nc.vector.tensor_tensor(new_sum[:, :], upd_ps[:, 2 * P:3 * P], old_sum[:, :], ALU.add)\
                  .then_inc(window_added, 1)

            def chunk(k, b, at):
                nxt = after(k, b)
                at_next = None if at is None else at + 1
                if has_next(at):
                    edge_rows(*nxt, at_next)
                    leftovers(*nxt, at_next)
                    edge_columns(*nxt, at_next)
                window_place(k, b, at)
                messages(k, b, at, 0)
                if from_chunk(at, 1):
                    add_window(2 * k + b - 1)
                messages(k, b, at, 1)

            edge_rows(0, 0, 0)
            leftovers(0, 0, 0)
            edge_columns(0, 0, 0)
            each_chunk(dve, chunk)
            add_window(CHUNKS - 1)

            nc.vector.tensor_reduce(valid_row[:, :], row_select[:, :], AX.X, ALU.add).then_inc(flag_step, 1)
            dve.wait_ge(left_ready, CHUNKS)
            nc.vector.tensor_reduce(missed_col[:, 0:1], missed_any[:, :], AX.X, ALU.max).then_inc(flag_step, 1)
            dve.wait_ge(flag_step, 2)
            nc.vector.tensor_scalar(missed_col[:, 1:2], missed_col[:, 0:1], 0.0, None, ALU.is_gt)\
              .then_inc(flag_step, 1)
            dve.wait_ge(flag_summed, 1)
            nc.vector.tensor_copy(flag[0:1, 0:1], row_ps[0:1, 0:1]).then_inc(flag_ready, 1)
            dve.wait_ge(flag_ready, 1)

            with dve.If(dve.value_load(flag[0:1, 0:1], min_val=0, max_val=P) > 0):
                with dve.Fori(0, EDGE_TILES) as i:
                    def vector_step(ins):
                        ins.then_inc(tile_vector, 1)

                    def made(name):
                        tile_step(dve, tile_vector, VECTOR_STEPS, i, name)

                    tile_step(dve, tile_tensor, TENSOR_STEPS, i, "lengths")
                    vector_step(nc.vector.tensor_scalar(r_clip[:, 0:P], row_ps[:, 0:P], 0.0, 1.0, ALU.max, ALU.min))
                    tile_step(dve, tile_scalar, SCALAR_STEPS, i, "gauss")
                    vector_step(nc.vector.scalar_tensor_tensor(emb[:, 0:P], row_ps[:, 0:P], 1.0, gauss[:, 0:P],
                                                               ALU.is_le, ALU.mult))
                    vector_step(nc.vector.tensor_tensor(one_norm[:, 0:1], one_square[:, 0:1], one_square[:, 1:2],
                                                        ALU.add))
                    made("norm_a")
                    vector_step(nc.vector.tensor_tensor(one_norm[:, 1:2], one_norm[:, 0:1], one_square[:, 2:3],
                                                        ALU.add))
                    tile_step(dve, tile_scalar, SCALAR_STEPS, i, "norm")
                    vector_step(nc.vector.tensor_scalar(one_norm[:, 3:4], one_norm[:, 2:3], 1e-12, None, ALU.add))
                    made("norm_eps")
                    vector_step(nc.vector.reciprocal(one_norm[:, 4:5], one_norm[:, 3:4]))
                    made("norm_inv")
                    vector_step(nc.vector.tensor_scalar(one_unit[:, :], one_attr[:, :], one_norm[:, 4:5], None,
                                                        ALU.mult))
                    dve.wait_ge(tile_loaded, 16 * TILE_LOADS * i + 16 * TILE_LOADS)
                    vector_step(nc.vector.tensor_copy(recv[:, :], one_left[:, :]))
                    made("recv")
                    vector_step(nc.vector.tensor_scalar(recv_diag[:, :], ident[:, :], recv[:, 0:1], None, ALU.mult))
                    tile_step(dve, tile_tensor, TENSOR_STEPS, i, "receivers")
                    vector_step(nc.vector.tensor_scalar(same[:, :], row_ps[:, P:2 * P], recv[:, 0:1], None,
                                                        ALU.is_equal))
                    made("same")
                    vector_step(nc.vector.tensor_tensor(same_earlier[:, :], same[:, :], earlier[:, :], ALU.mult))
                    made("same_earlier")
                    vector_step(nc.vector.tensor_reduce(repeated[:, 0:1], same_earlier[:, :], AX.X, ALU.max))
                    made("repeated")
                    vector_step(nc.vector.scalar_tensor_tensor(repeated[:, 1:2], pcol[:, :], float(NODES),
                                                               recv[:, :], ALU.add, ALU.subtract))
                    made("keep_first")
                    vector_step(nc.vector.scalar_tensor_tensor(target[:, :], repeated[:, 1:2], repeated[:, 0:1],
                                                               recv[:, :], ALU.mult, ALU.add))
                    dve.wait_ge(tile_rows, 16 * i + 16)
                    tile_step(dve, tile_scalar, SCALAR_STEPS, i, "weights")
                    m = msg[0][:, 0, :].rearrange("p (k f) -> p k f", f=MUL)
                    w = w_edge[0][:, 0, :].rearrange("p (k f) -> p k f", f=MUL)
                    xs = rows[0][0][:, 0, 0:MUL]
                    xv = rows[0][0][:, 0, MUL:FEAT].rearrange("p (c f) -> p c f", f=MUL)
                    y = spread(one_unit[:, :], 2, MUL)
                    vector_step(nc.vector.tensor_tensor(dot[:, 0, :, :], xv, y, ALU.mult))
                    vector_step(nc.vector.tensor_tensor(m[:, 0:9:8, :], w[:, 0:2, :], spread(xs, 1, 2), ALU.mult))
                    vector_step(nc.vector.tensor_tensor(m[:, 3:8:2, :], spread(w[:, 2, :], 1, 3), xv, ALU.mult))
                    made("scalar_blocks")
                    vector_step(nc.vector.tensor_tensor(dot_a[:, 0, :], dot[:, 0, 0, :], dot[:, 0, 1, :], ALU.add))
                    vector_step(nc.vector.tensor_tensor(m[:, 2:7:2, :], spread(m[:, 8, :], 1, 3), y, ALU.mult))
                    made("dot_a")
                    vector_step(nc.vector.tensor_tensor(dot_b[:, 0, :], dot_a[:, 0, :], dot[:, 0, 2, :], ALU.add))
                    made("dot_b")
                    vector_step(nc.vector.tensor_tensor(m[:, 1, :], dot_b[:, 0, :], w[:, 3, :], ALU.mult))
                    tile_step(dve, tile_tensor, TENSOR_STEPS, i, "update")
                    dve.wait_ge(tile_sums, 16 * i + 16)
                    vector_step(nc.vector.tensor_tensor(new_sum[:, :], upd_ps[:, 2 * P:3 * P], old_sum[:, :],
                                                        ALU.add))

            groups = NODE_TILES // LG
            seen = [0, 0]
            for g in range(groups):
                b = g % 2
                seen[b] += 16 if g < groups - 1 else 32
                dve.wait_ge(norm_loaded[b], seen[b])
                for t in range(LG):
                    last = nc.vector.bn_stats(ln_stat[:, t, :], ln_in[b][:, t, :])
                last.then_inc(ln_step, 1)
                dve.wait_ge(ln_step, 4 * g + 1)
                for t in range(LG):
                    last = nc.vector.bn_aggr(ln_mv[:, b, t, :], ln_stat[:, t, :])
                last.then_inc(ln_step, 1)
                dve.wait_ge(ln_step, 4 * g + 2)
                nc.vector.tensor_scalar(ln_eps[:, :], ln_mv[:, b, :, 1], 1e-5, None, ALU.add).then_inc(ln_var, 1)
                dve.wait_ge(ln_std, g + 1)
                nc.vector.tensor_tensor(ln_mid[:, :, :], ln_in[b][:, :, :], spread(ln_mv[:, b, :, 0], 2, FEAT),
                                        ALU.subtract).then_inc(ln_step, 1)
                nc.vector.reciprocal(ln_rs[:, :], ln_sd[:, :]).then_inc(ln_step, 1)
                dve.wait_ge(ln_step, 4 * g + 4)
                if g >= 2:
                    dve.wait_ge(out_saved[b], 16 * (g // 2))
                nc.vector.tensor_tensor(ln_out[b][:, :, :], ln_mid[:, :, :], spread(ln_rs[:, :], 2, FEAT),
                                        ALU.mult).then_inc(ln_ready, 1)


CONST_DMAS = 33
WUP = 9
W0_WIDE = 10
CONST_STEPS = 25

_INS = ["x", "src", "dst", "edge_attr_3", "edge_weight"] + [
    "L0_gnn_" + n for n in ("W_up0", "W_up1", "mlp_w0", "mlp_b0", "mlp_w1", "mlp_b1", "mlp_w2", "mlp_b2",
                            "W_out0", "W_out1")]


def kernel(**inputs):
    import numpy as np
    import concourse.bacc as bacc
    from concourse.bass_utils import run_bass_kernel_spmd as run

    nc = bacc.Bacc("TRN2", target_bir_lowering=False, num_devices=1)
    arrays, args = {}, []
    for name in _INS:
        a = np.ascontiguousarray(inputs[name])
        arrays[f"in_{name}"] = a
        args.append(nc.dram_tensor(f"in_{name}", a.shape, mybir.dt.from_np(a.dtype), kind="ExternalInput").ap())
    out = nc.dram_tensor("out_nodes", (NODES, FEAT), F32, kind="ExternalOutput").ap()
    build(nc, *args, out)
    r = run(nc, [arrays], core_ids=[0])
    return r.results[0]["out_nodes"]
```

```python
import math
from contextlib import ExitStack

import concourse.bass as bass
from concourse import mybir

F32 = mybir.dt.float32
BF16 = mybir.dt.bfloat16
I32 = mybir.dt.int32
ALU = mybir.AluOpType
ACT = mybir.ActivationFunctionType
AX = mybir.AxisListType

P = 128
NODES, EDGES, FEAT, MUL, CENTERS, HID = 12500, 400000, 128, 32, 8, 64
T = 14
V = 2 * T
HALF_V = V // 2
SUB = T * P
CHUNK = 2 * SUB
EDGE_TILES = EDGES // P
CHUNKS = -(-EDGE_TILES // V)
LAST_B = EDGE_TILES - (CHUNKS - 1) * V - T
WINDOW = 64
GROUP = CHUNK // 16
HCOL = 2 * GROUP
BLOCKS = 9
MSG = 256
NODE_TILES = -(-NODES // P)
LAST_NODES = NODES - (NODE_TILES - 1) * P
NG = 4
NODE_GROUPS = NODE_TILES // NG
SHORT = NODE_TILES - NODE_GROUPS * NG
RING = 4
LAG = 16
EARLY = CHUNKS - LAG
TAIL = NODE_TILES - EARLY
END_PARTS = ((0, 8, 2), (8, HALF_V, 2))
assert 2 * LAST_B <= HALF_V and CHUNKS % 2 == 0 and NODE_GROUPS % RING == 0 and LAG % 2 == 0


def spread(ap, axis, n):
    shape = list(ap.shape)
    shape.insert(axis, n)
    return ap.unsqueeze(axis).broadcast_to(shape)


def build(nc, x, src, dst, edge_attr_3, edge_weight, W_up0, W_up1, mlp_w0, mlp_b0, mlp_w1, mlp_b1,
          mlp_w2, mlp_b2, W_out0, W_out1, out):
    src2 = src.rearrange("(t p) -> t p", p=P)
    dst2 = dst.rearrange("(t p) -> t p", p=P)
    attr2 = edge_attr_3.rearrange("(t p) c -> t (p c)", p=P)
    dst_flat = dst.rearrange("(a n) -> a n", a=1)
    r_flat = edge_weight

    ctx = ExitStack()
    with ctx:
        def sb(name, shape, dt=F32):
            return ctx.enter_context(nc.sbuf_tensor(name, shape, dt))

        def ps(name, shape=(P, 512)):
            return ctx.enter_context(nc.psum_tensor(name, list(shape), F32))

        def sem(name):
            return ctx.enter_context(nc.semaphore(name))

        table = nc.dram_tensor("projected", (NODES, FEAT), F32).ap()
        node_sum = nc.dram_tensor("node_sum", (NODES + P, FEAT), F32).ap()
        leftover = nc.dram_tensor("leftover", (EDGE_TILES, P), I32).ap()

        iota_i = sb("iota_i", [P, P], I32)
        pcol_i = sb("pcol_i", [P, 3], I32)
        iota_f = sb("iota_f", [P, P])
        trash_row = sb("trash_row", [P, P])
        pcol = sb("pcol", [P, 1])
        window_lane = sb("window_lane", [P, 1])
        minus_center = sb("minus_center", [P, 1])
        ident = sb("ident", [P, P])
        group_rep = sb("group_rep", [P, P])
        group_low = sb("group_low", [P, P])
        row_select = sb("row_select", [P, V])
        lane_center_i = sb("lane_center_i", [P, P], I32)
        lane_center = sb("lane_center", [P, P])
        center_rows = sb("center_rows", [CENTERS, P])
        w0_raw = sb("w0_raw", [CENTERS, HID])
        w0_wide = sb("w0_wide", [P, 8, 2, HID])
        w0_keep = sb("w0_keep", [P, 8, 2, HID])
        w0_groups = sb("w0_groups", [P, 8, 2, HID])
        w1_diag = sb("w1_diag", [P, P])
        w2_diag = sb("w2_diag", [P, 2 * P])
        bias01 = sb("bias01", [P, 2])
        b2_rep = sb("b2_rep", [P, P])
        b2_part = sb("b2_part", [P, 3, P], BF16)
        b2_rest = sb("b2_rest", [P, 2, P])
        b2_mask = sb("b2_mask", [P, 3])
        b2_sum = sb("b2_sum", [P, 2, P])
        b2_rows = sb("b2_rows", [P, 4, P], BF16)
        ones_bf = sb("ones_bf", [P, P], BF16)
        wup_raw = sb("wup_raw", [P, P])
        wup = sb("wup", [P, P])
        wout_raw = sb("wout_raw", [P, 2, MUL])
        wout_scale = sb("wout_scale", [P, 2])
        wout = sb("wout", [P, 2, P])
        zeros = sb("zeros", [P, P])

        x_ring = sb("x_ring", [P, RING, NG, P])
        xT = sb("xT", [P, 2, NG * P])
        proj = sb("proj", [P, RING, NG * P])

        src_row = [sb(f"src_row{b}", [P, P], I32) for b in range(2)]
        dst_row = [sb(f"dst_row{b}", [P, P], I32) for b in range(2)]
        attr_row = [sb(f"attr_row{b}", [P, P, 3]) for b in range(2)]
        base = [sb(f"base{b}", [P, 2], I32) for b in range(2)]
        r_in = [sb(f"r_in{b}", [P, GROUP]) for b in range(2)]
        src_f = sb("src_f", [P, P])
        rel = sb("rel", [P, P])
        window_out = sb("window_out", [P, P])
        chunk_rel = sb("chunk_rel", [P, P])
        chunk_out = sb("chunk_out", [P, P])
        missed = sb("missed", [P, P])
        missed_any = sb("missed_any", [P, P])
        above_trash = sb("above_trash", [P, P])
        missed_row = sb("missed_row", [P, P])
        left_row = [sb(f"left_row{b}", [P, P], I32) for b in range(2)]
        window_node = [sb(f"window_node{b}", [P, 1]) for b in range(2)]
        idx = [sb(f"idx{b}", [P, V], I32) for b in range(2)]
        one_hot = [sb(f"one_hot{b}", [P, V, WINDOW]) for b in range(2)]
        square = sb("square", [P, 3, V])
        norm_a = sb("norm_a", [P, V])
        norm2 = sb("norm2", [P, V])
        norm = sb("norm", [P, V])
        norm_eps = sb("norm_eps", [P, V])
        norm_inv = sb("norm_inv", [P, V])
        unit = [sb(f"unit{b}", [P, 3, V]) for b in range(2)]

        r_clip = sb("r_clip", [P, GROUP])
        gauss_arg = sb("gauss_arg", [P, GROUP])
        gauss = sb("gauss", [P, GROUP])
        emb = sb("emb", [P, GROUP])
        h1 = sb("h1", [P, SUB])
        h2 = [sb(f"h2_{b}", [P, SUB]) for b in range(2)]
        w_edge = [sb(f"w_edge{h}", [P, HALF_V, P]) for h in range(2)]

        rows = [[sb(f"rows{b}{h}", [P, HALF_V, FEAT]) for h in range(2)] for b in range(2)]
        msg = [sb(f"msg{h}", [P, HALF_V, BLOCKS * MUL]) for h in range(2)]
        dot = sb("dot", [P, HALF_V, 3, MUL])
        dot_a = sb("dot_a", [P, HALF_V, MUL])
        dot_b = sb("dot_b", [P, HALF_V, MUL])

        place = [sb(f"place{b}", [P, P]) for b in range(2)]
        win_sb = sb("win_sb", [P, MSG])
        nodesT = sb("nodesT", [P, MSG])
        old_sum = sb("old_sum", [P, P])
        new_sum = sb("new_sum", [P, P])

        one_src = sb("one_src", [P, 1], I32)
        one_left = sb("one_left", [P, 1], I32)
        one_attr = sb("one_attr", [P, 3])
        one_square = sb("one_square", [P, 3])
        one_norm = sb("one_norm", [P, 5])
        one_unit = sb("one_unit", [P, 3])
        recv = sb("recv", [P, 1])
        recv_diag = sb("recv_diag", [P, P])
        same = sb("same", [P, P])
        same_earlier = sb("same_earlier", [P, P])
        earlier = sb("earlier", [P, P])
        repeated = sb("repeated", [P, 3])
        target = sb("target", [P, 1], I32)
        ones = sb("ones", [P, P])
        valid_row = sb("valid_row", [P, 1])
        missed_col = sb("missed_col", [P, 4])
        flag = sb("flag", [1, 2], I32)

        ln_in = [sb(f"ln_in{b}", [P, P]) for b in range(TAIL)]
        ln_out = [sb(f"ln_out{b}", [P, P]) for b in range(TAIL)]
        ln_stat = sb("ln_stat", [P, 6])
        ln_mv = sb("ln_mv", [P, 2])
        ln_var = sb("ln_var", [P, 1])
        ln_sd = sb("ln_sd", [P, 1])
        ln_rs = sb("ln_rs", [P, 1])
        chunk_start = [sb(f"chunk_start{b}", [P, 1]) for b in range(2)]
        normed_end = sb("normed_end", [P, 1])
        reach_back = sb("reach_back", [P, 2])

        hid_ps = [ps(f"hid_ps{i}") for i in range(2)]
        w_ps = [ps(f"w_ps{i}") for i in range(2)]
        row_ps = ps("row_ps")
        win_ps = ps("win_ps")
        upd_ps = ps("upd_ps")

        const_loaded = sem("const_loaded")
        const_pool = sem("const_pool")
        const_step = sem("const_step")
        x_loaded = [sem(f"x_loaded{i}") for i in range(RING)]
        sums_started = sem("sums_started")
        wup_loaded = sem("wup_loaded")
        w0_loaded = sem("w0_loaded")
        w0_repeated = sem("w0_repeated")
        xT_ready = sem("xT_ready")
        xT_copied = sem("xT_copied")
        proj_ready = sem("proj_ready")
        proj_copied = sem("proj_copied")
        proj_saved = [sem(f"proj_saved{i}") for i in range(RING)]
        rows_loaded = [sem(f"rows_loaded{b}") for b in range(2)]
        rows_ready = sem("rows_ready")
        edge_scalars = sem("edge_scalars")
        clip_ready = sem("clip_ready")
        gauss_step = sem("gauss_step")
        emb_ready = sem("emb_ready")
        left_step = sem("left_step")
        left_ready = sem("left_ready")
        left_saved = [sem(f"left_saved{b}") for b in range(2)]
        transposed = sem("transposed")
        squared = sem("squared")
        norm_step = sem("norm_step")
        norm2_ready = sem("norm2_ready")
        norm_ready = sem("norm_ready")
        idx_ready = sem("idx_ready")
        one_hot_ready = sem("one_hot_ready")
        unit_ready = sem("unit_ready")
        end_gathered = sem("end_gathered")
        rows_free = sem("rows_free")
        gathered = [[sem(f"gathered{b}{h}") for h in range(2)] for b in range(2)]
        hid_ready = sem("hid_ready")
        hid_copied = sem("hid_copied")
        w_ready = sem("w_ready")
        w_copied = sem("w_copied")
        msg_step = sem("msg_step")
        msg_ready = sem("msg_ready")
        msg_summed = sem("msg_summed")
        win_copied = sem("win_copied")
        place_ready = sem("place_ready")
        placed = sem("placed")
        placed_copied = sem("placed_copied")
        upd_ready = sem("upd_ready")
        window_read = sem("window_read")
        window_added = sem("window_added")
        window_saved = sem("window_saved")
        flag_step = sem("flag_step")
        flag_summed = sem("flag_summed")
        flag_ready = sem("flag_ready")
        tile_loaded = sem("tile_loaded")
        tile_vector = sem("tile_vector")
        tile_scalar = sem("tile_scalar")
        tile_tensor = sem("tile_tensor")
        tile_rows = sem("tile_rows")
        tile_sums = sem("tile_sums")
        tile_saved = sem("tile_saved")
        tile_done = sem("tile_done")
        start_known = sem("start_known")
        reach_step = sem("reach_step")
        ln_loaded = [sem(f"ln_loaded{b}") for b in range(2)]
        ln_slot_free = sem("ln_slot_free")
        ln_saved = [sem(f"ln_saved{b}") for b in range(2)]
        turn_ln = [sem(f"turn_ln_{n}") for n in ("stats", "variance", "deviation", "inverse", "result")]
        again_ln = [sem(f"again_ln_{n}") for n in ("stats", "variance", "deviation", "inverse", "result")]
        tail_ln = [sem(f"tail_ln_{n}") for n in ("stats", "variance", "deviation", "inverse", "result")]
        again_loaded = sem("again_loaded")
        again_saved = sem("again_saved")
        again_next = sem("again_next")
        tail_loaded = sem("tail_loaded")
        tail_saved = sem("tail_saved")

        LOADS_PER = 10

        def each_chunk(eng, body):
            for c in (0, 1):
                body(c // 2, c % 2, c, False)
            with eng.Fori(1, LAG // 2) as k:
                body(k, 0, None, False)
                body(k, 1, None, False)
            with eng.Fori(LAG // 2, CHUNKS // 2 - 2) as k:
                body(k, 0, None, True)
                body(k, 1, None, True)
            for c in range(CHUNKS - 4, CHUNKS):
                body(c // 2, c % 2, c, True)

        def after(k, b, steps=1):
            return (k + (b + steps) // 2, (b + steps) % 2)

        def from_chunk(at, n):
            return at is None or at >= n

        def has_next(at, steps=1):
            return at is None or at + steps < CHUNKS

        def loaded_count(k, at):
            return 16 * LOADS_PER * (k + 1) + (16 if at == CHUNKS - 1 else 0)

        def sub_rows(b_tiles):
            return ((0, 0, T), (WINDOW, T, b_tiles))

        def last_tiles(at, h):
            return [v for v in range(h * HALF_V, (h + 1) * HALF_V)
                    if at != CHUNKS - 1 or v % 2 == 0 or v // 2 < LAST_B]

        VECTOR_STEPS = ("clip", "embedding", "norm_a", "norm2", "norm_eps", "norm_inv", "unit", "recv",
                        "recv_diag", "same", "same_earlier", "repeated", "keep_first", "target", "dot",
                        "scalar_blocks", "vector_blocks", "dot_a", "unit_blocks", "dot_b", "dot_block", "sum")
        SCALAR_STEPS = ("square", "gauss_arg", "gauss", "norm", "hidden0", "hidden1", "weights", "placed")
        TENSOR_STEPS = ("lengths", "receivers", "hidden0", "hidden1", "weights", "placed", "update")
        TILE_LOADS = 4

        def tile_step(eng, signal, steps, i, name):
            eng.wait_ge(signal, i * len(steps) + steps.index(name) + 1)

        hidden_seq = 2 * (SUB // HCOL)
        assert hidden_seq == 8 and HALF_V * P == 4 * 512 - 256
        W_GROUPS = 4

        block = ctx.enter_context(nc.Block())

        @block.sync
        def _(sp):
            def load_rows(k, b, at):
                c = 2 * k + b
                b_tiles = LAST_B if at == CHUNKS - 1 else T
                if from_chunk(at, 2):
                    sp.wait_ge(edge_scalars, c - 1)
                    sp.wait_ge(left_ready, c - 1)
                    sp.wait_ge(transposed, c - 1)
                done = rows_loaded[b]
                for p0, t0, n in sub_rows(b_tiles):
                    first = c * V + t0
                    sp.dma_start(src_row[b][p0:p0 + n, :], src2[bass.ds(first, n), :]).then_inc(done, 16)
                    sp.dma_start(dst_row[b][p0:p0 + n, :], dst2[bass.ds(first, n), :]).then_inc(done, 16)
                    sp.dma_start(attr_row[b][p0:p0 + n, :, :].rearrange("t p c -> t (p c)"),
                                 attr2[bass.ds(first, n), :]).then_inc(done, 16)
                with nc.allow_non_contiguous_dma(reason="one receiver to every partition"):
                    for s in range(2):
                        sub0 = dst_flat[:, bass.ds(c * CHUNK + s * SUB, 1)]
                        sp.dma_start(base[b][s * WINDOW:(s + 1) * WINDOW, 0:1],
                                     sub0.broadcast_to([WINDOW, 1])).then_inc(done, 16)
                    sp.dma_start(base[b][:, 1:2], dst_flat[:, bass.ds(c * CHUNK, 1)].broadcast_to([P, 1]))\
                      .then_inc(done, 16)
                if at != CHUNKS - 1:
                    r = r_flat[bass.ds(c * CHUNK, CHUNK)].rearrange("(g j) -> g j", g=16)
                    sp.dma_start(r_in[b][0:16, :], r).then_inc(done, 16)
                else:
                    edges = EDGES - c * CHUNK
                    whole, rest = edges // GROUP, edges % GROUP
                    r = r_flat[c * CHUNK:c * CHUNK + whole * GROUP].rearrange("(g j) -> g j", g=whole)
                    sp.dma_start(r_in[b][0:whole, :], r).then_inc(done, 16)
                    r = r_flat[c * CHUNK + whole * GROUP:EDGES].rearrange("(a j) -> a j", a=1)
                    sp.dma_start(r_in[b][whole:whole + 1, 0:rest], r).then_inc(done, 16)

            def const(dst_ap, src_ap, signal=const_loaded):
                sp.dma_start(dst_ap, src_ap).then_inc(signal, 16)

            def save_group(g, ring):
                sp.wait_ge(proj_copied, g + 1)
                where = table[bass.ds(g * NG * P, NG * P), :].rearrange("(t p) f -> p t f", p=P)
                sp.dma_start(where, proj[:, ring, :].rearrange("p (t f) -> p t f", f=P))\
                  .then_inc(proj_saved[ring], 16)

            sp.wait_ge(const_step, 1)
            const(wup_raw[0:MUL, 0:MUL], W_up0, wup_loaded)
            for c in range(3):
                const(wup_raw[MUL + c:MUL + c + 3 * (MUL - 1) + 1:3, MUL * (c + 1):MUL * (c + 2)], W_up1,
                      wup_loaded)
            load_rows(0, 0, 0)
            const(w0_raw[:, :], mlp_w0, w0_loaded)
            save_group(0, 0)
            for s in range(2):
                const(w1_diag[s * HID:(s + 1) * HID, s * HID:(s + 1) * HID], mlp_w1)
                const(w2_diag[s * HID:(s + 1) * HID, s * P:(s + 1) * P], mlp_w2)
            save_group(1, 1)
            for s in range(2):
                with nc.allow_non_contiguous_dma(reason="biases"):
                    const(bias01[s * HID:(s + 1) * HID, 0:1], mlp_b0.rearrange("(p a) -> p a", a=1))
                    const(bias01[s * HID:(s + 1) * HID, 1:2], mlp_b1.rearrange("(p a) -> p a", a=1))
            save_group(2, 2)
            const(b2_rep[:, :], mlp_b2.rearrange("(a n) -> a n", a=1).broadcast_to([P, P]))
            const(wout_raw[0:HID, 0, :], W_out0)
            const(wout_raw[HID:P, 0, :], W_out1)
            const(wout_raw[0:HID, 1, :], W_out1)
            const(wout_raw[HID:P, 1, :], W_out1)
            save_group(3, 3)
            with sp.Fori(1, NODE_GROUPS // RING) as k:
                for ring in range(RING):
                    save_group(RING * k + ring, ring)
            row = NODE_GROUPS * NG * P
            sp.wait_ge(proj_copied, NODE_GROUPS + 1)
            sp.dma_start(table[row:row + P, :], proj[:, 0, 0:P]).then_inc(proj_saved[0], 16)
            sp.dma_start(table[row + P:NODES, :], proj[0:LAST_NODES, 0, P:2 * P]).then_inc(proj_saved[0], 16)

            load_rows(0, 1, 1)
            sp.dma_start(node_sum[0:NODES, :].rearrange("n f -> (n f)").rearrange("(a b) -> a b", a=P),
                         x.rearrange("n f -> (n f)").rearrange("(a b) -> a b", a=P)).then_inc(sums_started, 16)
            sp.dma_start(node_sum[NODES:NODES + P, :], zeros[:, :]).then_inc(sums_started, 16)

            def chunk(k, b, at, norms):
                c = 2 * k + b
                b_tiles = LAST_B if at == CHUNKS - 1 else T
                first_node = sp.value_load(dst_flat[0:1, bass.ds(c * CHUNK, 1)], min_val=0, max_val=NODES - 1)
                if has_next(at, 2):
                    load_rows(k + 1, b, None if at is None else at + 2)
                if from_chunk(at, 1):
                    sp.wait_ge(window_saved, 16 * c)
                else:
                    sp.wait_ge(sums_started, 32)
                if norms:
                    sp.dma_start(ln_in[b][:, :], node_sum[bass.ds((c - LAG) * P, P), :]).then_inc(ln_loaded[b], 16)
                window = node_sum[bass.ds(first_node, P), :]
                sp.dma_start(old_sum[:, :], window).then_inc(window_read, 16)
                sp.wait_ge(left_ready, c + 1)
                for p0, t0, n in sub_rows(b_tiles):
                    sp.dma_start(leftover[bass.ds(c * V + t0, n), :], left_row[b][p0:p0 + n, :])\
                      .then_inc(left_saved[b], 16)
                if norms:
                    sp.wait_ge(turn_ln[4], c - LAG + 1)
                    sp.dma_start(out[bass.ds((c - LAG) * P, P), :], ln_out[b][:, :]).then_inc(ln_saved[b], 16)
                sp.wait_ge(window_added, c + 1)
                sp.dma_start(window, new_sum[:, :]).then_inc(window_saved, 16)
                if norms:
                    sp.wait_ge(ln_saved[b], 16 * (k - LAG // 2 + 1))
                    sp.sem_inc(ln_slot_free, 1)

            each_chunk(sp, chunk)

            sp.wait_ge(window_saved, 16 * CHUNKS)
            for b in range(2):
                sp.wait_ge(left_saved[b], 16 * CHUNKS)
                sp.wait_ge(ln_saved[b], 16 * EARLY // 2)
            sp.wait_ge(flag_ready, 1)
            with sp.If(sp.value_load(flag[0:1, 0:1], min_val=0, max_val=P) > 0):
                with sp.Fori(0, EDGE_TILES) as i:
                    with nc.allow_non_contiguous_dma(reason="one edge to every partition"):
                        sp.dma_start(one_src[:, :], src2[bass.ds(i, 1), :].rearrange("a p -> p a"))\
                          .then_inc(tile_loaded, 16)
                        sp.dma_start(one_left[:, :], leftover[bass.ds(i, 1), :].rearrange("a p -> p a"))\
                          .then_inc(tile_loaded, 16)
                    sp.dma_start(one_attr[:, :], attr2[bass.ds(i, 1), :].rearrange("a (p c) -> (a p) c", c=3))\
                      .then_inc(tile_loaded, 16)
                    sp.dma_start(r_in[0][0:1, 0:P], r_flat[bass.ds(i * P, P)].rearrange("(a j) -> a j", a=1))\
                      .then_inc(tile_loaded, 16)
                    sp.wait_ge(tile_saved, 16 * i + 16)
                    sp.sem_inc(tile_done, 1)
            with sp.If(sp.value_load(flag[0:1, 1:2], min_val=0, max_val=P) > 0):
                with sp.Fori(0, EARLY) as i:
                    sp.dma_start(ln_in[0][:, :], node_sum[bass.ds(i * P, P), :]).then_inc(again_loaded, 16)
                    sp.wait_ge(again_ln[4], i + 1)
                    sp.dma_start(out[bass.ds(i * P, P), :], ln_out[0][:, :]).then_inc(again_saved, 16)
                    sp.wait_ge(again_saved, 16 * i + 16)
                    sp.sem_inc(again_next, 1)

            for i in range(TAIL):
                row = (EARLY + i) * P
                sp.dma_start(ln_in[i][:, :], node_sum[row:row + P, :]).then_inc(tail_loaded, 16)
            for i in range(TAIL):
                row = (EARLY + i) * P
                n = min(P, NODES - row)
                sp.wait_ge(tail_ln[4], i + 1)
                sp.dma_start(out[row:row + n, :], ln_out[i][0:n, :]).then_inc(tail_saved, 16)
            sp.wait_ge(tail_saved, 16 * TAIL)

        @block.gpsimd
        def _(pool):
            n_pool = [0]

            def step(ins):
                ins.then_inc(const_pool, 1)
                n_pool[0] += 1
                return n_pool[0]

            step(nc.gpsimd.iota(iota_i[:, :], pattern=[[1, P]], base=0, channel_multiplier=0))
            step(nc.gpsimd.iota(pcol_i[:, 0:1], pattern=[[1, 1]], base=0, channel_multiplier=1))
            step(nc.gpsimd.memset(ident[:, :], 0.0))
            step(nc.gpsimd.memset(group_low[:, :], 1.0))
            n = step(nc.gpsimd.memset(row_select[:, :], 0.0))
            pool.wait_ge(const_pool, n)
            step(nc.gpsimd.affine_select(out=ident[:, :], in_=ident[:, :], compare_op=ALU.not_equal, fill=1.0,
                                         base=0, pattern=[[-1, P]], channel_multiplier=1))
            sel = row_select[:, :].rearrange("p (t s) -> p t s", s=2)
            step(nc.gpsimd.affine_select(out=sel, in_=sel, compare_op=ALU.not_equal, fill=1.0, base=0,
                                         pattern=[[-1, T], [-WINDOW, 2]], channel_multiplier=1))
            pool.wait_ge(const_step, 1)
            n = step(nc.gpsimd.affine_select(out=group_low[:, :], in_=group_low[:, :], compare_op=ALU.is_ge,
                                             fill=0.0, base=0, pattern=[[1, P]], channel_multiplier=-CENTERS))
            pool.wait_ge(const_pool, n)
            step(nc.gpsimd.affine_select(out=group_rep[:, :], in_=group_low[:, :], compare_op=ALU.is_ge,
                                         fill=0.0, base=CENTERS - 1, pattern=[[-1, P]],
                                         channel_multiplier=CENTERS))
            step(nc.gpsimd.affine_select(out=earlier[:, :], in_=ones[:, :], compare_op=ALU.is_gt, fill=0.0,
                                         base=0, pattern=[[-1, P]], channel_multiplier=1))
            pool.wait_ge(const_step, W0_WIDE)
            pattern = [[-CENTERS, 8], [-HID, 2], [0, HID]]
            n = step(nc.gpsimd.affine_select(out=w0_keep[:, :, :, :], in_=w0_wide[:, :, :, :],
                                             compare_op=ALU.is_ge, fill=0.0, base=0, pattern=pattern,
                                             channel_multiplier=1))
            pool.wait_ge(const_pool, n)
            pattern = [[CENTERS, 8], [HID, 2], [0, HID]]
            step(nc.gpsimd.affine_select(out=w0_groups[:, :, :, :], in_=w0_keep[:, :, :, :],
                                         compare_op=ALU.is_ge, fill=0.0, base=CENTERS - 1, pattern=pattern,
                                         channel_multiplier=-1))

            for ring in range(RING):
                pool.wait_ge(proj_saved[ring], 16 * (NODE_GROUPS // RING) + (32 if ring == 0 else 0))

            def chunk(k, b, at, norms):
                c = 2 * k + b
                pool.wait_ge(idx_ready, c + 1)
                for h in range(2):
                    if from_chunk(at, 2):
                        pool.wait_ge(msg_ready, 2 * (c - 2) + h + 1)
                        pool.sem_inc(rows_free, 1)
                    for v in last_tiles(at, h):
                        at_end = at == CHUNKS - 1 and h == 1 and v - HALF_V >= END_PARTS[1][0]
                        pool.indirect_dma_start(rows[b][h][:, v - h * HALF_V, :], None, table[:, :],
                                                bass.IndirectOffsetOnAxis(ap=idx[b][:, v:v + 1], axis=0))\
                            .then_inc(end_gathered if at_end else gathered[b][h], 16)

            each_chunk(pool, chunk)

            pool.wait_ge(flag_ready, 1)
            with pool.If(pool.value_load(flag[0:1, 0:1], min_val=0, max_val=P) > 0):
                with pool.Fori(0, EDGE_TILES) as i:
                    pool.wait_ge(tile_loaded, 16 * TILE_LOADS * i + 16 * TILE_LOADS)
                    pool.sem_inc(rows_free, 1)
                    pool.indirect_dma_start(rows[0][0][:, 0, :], None, table[:, :],
                                            bass.IndirectOffsetOnAxis(ap=one_src[:, :], axis=0))\
                        .then_inc(tile_rows, 16)
                    pool.indirect_dma_start(old_sum[:, :], None, node_sum[:, :],
                                            bass.IndirectOffsetOnAxis(ap=one_left[:, :], axis=0))\
                        .then_inc(tile_sums, 16)
                    tile_step(pool, tile_vector, VECTOR_STEPS, i, "sum")
                    pool.sem_inc(rows_free, 1)
                    pool.indirect_dma_start(node_sum[:, :], bass.IndirectOffsetOnAxis(ap=target[:, :], axis=0),
                                            new_sum[:, :], None).then_inc(tile_saved, 16)

        @block.tensor
        def _(pe):
            pe.wait_ge(const_pool, 6)

            def transpose_nodes(g, ring, loaded, tiles, first=False):
                pe.wait_ge(x_loaded[ring], loaded)
                if not first:
                    pe.wait_ge(xT_copied, g - 1)
                for i, n in enumerate(tiles):
                    last = nc.tensor.transpose(hid_ps[ring % 2][:, i * P:i * P + n], x_ring[0:n, ring, i, :],
                                               ident[0:n, 0:n])
                last.then_inc(xT_ready, 1)

            def project_nodes(g, half, tiles, first=False):
                pe.wait_ge(xT_copied, g + 1)
                if not first:
                    pe.wait_ge(proj_copied, g - 1)
                for i, n in enumerate(tiles):
                    last = nc.tensor.matmul(w_ps[half][0:n, i * P:(i + 1) * P], xT[:, half, i * P:i * P + n],
                                            wup[:, :], start=True, stop=True)
                last.then_inc(proj_ready, 1)

            whole = [P] * NG
            short = [P] * (SHORT - 1) + [LAST_NODES]
            for ring in range(RING):
                transpose_nodes(ring, ring, 16, whole, first=ring < 2)
                if ring == 1:
                    pe.wait_ge(const_step, WUP)
                if ring >= 1:
                    project_nodes(ring - 1, (ring - 1) % 2, whole, first=ring < 3)

            def transpose_rows(k, b, at):
                c = 2 * k + b
                pe.wait_ge(rows_ready, c + 1)
                pe.wait_ge(rows_loaded[b], loaded_count(k, at))
                if from_chunk(at, 1):
                    pe.wait_ge(unit_ready, c)
                    pe.wait_ge(one_hot_ready, c)
                    pe.wait_ge(emb_ready, c)
                for i, lhs in enumerate([src_f[:, :], rel[:, :]] + [attr_row[b][:, :, j] for j in range(3)]):
                    last = nc.tensor.matmul(row_ps[:, i * V:(i + 1) * V], lhs, row_select[:, :],
                                            start=True, stop=True)
                last = nc.tensor.matmul(row_ps[:, 5 * V:5 * V + GROUP], group_rep[:, :], r_in[b][:, :],
                                        start=True, stop=True)
                last.then_inc(transposed, 1)

            pe.wait_ge(const_pool, 10)
            transpose_rows(0, 0, 0)
            pe.wait_ge(w0_loaded, 16)
            nc.tensor.matmul(win_ps[:, 0:HID], center_rows[:, :], w0_raw[:, :], start=True, stop=True)\
              .then_inc(w0_repeated, 1)
            with pe.Fori(1, NODE_GROUPS // RING) as k:
                for ring in range(RING):
                    g = RING * k + ring
                    transpose_nodes(g, ring, 16 * (k + 1), whole)
                    project_nodes(g - 1, (ring - 1) % 2, whole)
            transpose_nodes(NODE_GROUPS, 0, 16 * (NODE_GROUPS // RING) + 32, short)
            project_nodes(NODE_GROUPS - 1, 1, whole)
            project_nodes(NODE_GROUPS, 0, short)
            pe.wait_ge(xT_copied, NODE_GROUPS + 1)
            pe.wait_ge(proj_copied, NODE_GROUPS + 1)
            pe.wait_ge(const_step, CONST_STEPS)
            pe.wait_ge(const_pool, 12)

            def hidden(k, b, at, layer):
                c = 2 * k + b
                if layer == 0:
                    pe.wait_ge(emb_ready, c + 1)
                for i in range(4):
                    n = 4 * layer + i
                    if from_chunk(at, 1) or n >= 2:
                        pe.wait_ge(hid_copied, 8 * c + n - 1)
                    bank = hid_ps[n % 2]
                    if layer == 0:
                        for j in range(2):
                            q = 2 * i + j
                            last = nc.tensor.matmul(bank[:, j * GROUP:(j + 1) * GROUP],
                                                    w0_groups[:, q, :, :].rearrange("p s f -> p (s f)"),
                                                    emb[:, :], start=True, stop=True)
                    else:
                        last = nc.tensor.matmul(bank[:, 0:HCOL], w1_diag[:, :], h1[:, i * HCOL:(i + 1) * HCOL],
                                                start=True, stop=True)
                    last.then_inc(hid_ready, 1)

            def edge_weights(k, b, at, h):
                c = 2 * k + b
                pe.wait_ge(hid_copied, 8 * c + 8)
                for i in range(W_GROUPS):
                    m = h * W_GROUPS + i
                    if from_chunk(at, 1) or m >= 2:
                        pe.wait_ge(w_copied, 8 * c + m - 1)
                    bank = w_ps[m % 2]
                    pairs = range(7 * h + 2 * i, min(7 * h + 2 * i + 2, 7 * h + 7))
                    width = 2 * P * len(pairs)
                    nc.tensor.matmul(bank[:, 0:width], ones_bf[:, :],
                                     b2_rows[:, 0:2 * len(pairs), :].rearrange("p a f -> p (a f)"),
                                     start=True, stop=False)
                    for j, t in enumerate(pairs):
                        last = nc.tensor.matmul(bank[:, 2 * P * j:2 * P * (j + 1)], h2[b][:, t * P:(t + 1) * P],
                                                w2_diag[:, :], start=False, stop=j == len(pairs) - 1)
                    last.then_inc(w_ready, 1)

            def sum_messages(k, b, at, h):
                c = 2 * k + b
                pe.wait_ge(msg_ready, 2 * c + h + 1)
                ends_in_parts = at == CHUNKS - 1 and h == 1
                if h == 0:
                    pe.wait_ge(one_hot_ready, c + 1)
                    if from_chunk(at, 1):
                        pe.wait_ge(win_copied, c)
                ends = [max(v for v in last_tiles(at, 0) + last_tiles(at, 1) if v % 2 == s) for s in range(2)]
                for v in last_tiles(at, h):
                    if ends_in_parts and v - HALF_V == END_PARTS[1][0]:
                        pe.wait_ge(msg_ready, 2 * c + h + 2)
                    s = v % 2
                    last = nc.tensor.matmul(win_ps[s * WINDOW:(s + 1) * WINDOW, 0:MSG], one_hot[b][:, v, :],
                                            msg[h][:, v - h * HALF_V, 0:MSG], start=v < 2, stop=v == ends[s])
                last.then_inc(msg_summed, 1)

            def place_windows(k, b):
                c = 2 * k + b
                pe.wait_ge(win_copied, c + 1)
                pe.wait_ge(place_ready, c + 1)
                for j in range(2):
                    last = nc.tensor.matmul(upd_ps[:, j * P:(j + 1) * P], win_sb[:, j * P:(j + 1) * P],
                                            place[b][:, :], start=True, stop=True)
                last.then_inc(placed, 1)

            def project_out(k, b, at):
                c = 2 * k + b
                pe.wait_ge(placed_copied, c + 1)
                if from_chunk(at, 1):
                    pe.wait_ge(window_added, c)
                for j in range(2):
                    last = nc.tensor.matmul(upd_ps[:, 2 * P:3 * P], nodesT[:, j * P:(j + 1) * P],
                                            wout[:, j, :], start=j == 0, stop=j == 1)
                last.then_inc(upd_ready, 1)

            def back(k, b):
                return (k, 0) if b else (k - 1, 1)

            def chunk(k, b, at, norms):
                nxt = after(k, b)
                at_next = None if at is None else at + 1
                if has_next(at):
                    transpose_rows(*nxt, at_next)
                edge_weights(k, b, at, 1)
                if from_chunk(at, 1):
                    place_windows(*back(k, b))
                if has_next(at):
                    hidden(*nxt, at_next, 0)
                if from_chunk(at, 1):
                    project_out(*back(k, b), None if at is None else at - 1)
                if has_next(at):
                    hidden(*nxt, at_next, 1)
                sum_messages(k, b, at, 0)
                if has_next(at):
                    edge_weights(*nxt, at_next, 0)
                sum_messages(k, b, at, 1)

            hidden(0, 0, 0, 0)
            hidden(0, 0, 0, 1)
            edge_weights(0, 0, 0, 0)
            each_chunk(pe, chunk)
            k, b = (CHUNKS - 1) // 2, (CHUNKS - 1) % 2
            place_windows(k, b)
            pe.wait_ge(flag_step, 5)
            nc.tensor.matmul(row_ps[0:1, 0:2], valid_row[:, :], missed_col[:, 1:3], start=True, stop=True)\
              .then_inc(flag_summed, 1)
            project_out(k, b, CHUNKS - 1)
            pe.wait_ge(flag_ready, 1)
            with pe.If(pe.value_load(flag[0:1, 0:1], min_val=0, max_val=P) > 0):
                with pe.Fori(0, EDGE_TILES) as i:
                    pe.wait_ge(tile_loaded, 16 * TILE_LOADS * i + 16 * TILE_LOADS)
                    nc.tensor.matmul(row_ps[:, 0:P], group_rep[:, :], r_in[0][:, 0:P], start=True, stop=True)\
                      .then_inc(tile_tensor, 1)
                    tile_step(pe, tile_vector, VECTOR_STEPS, i, "recv_diag")
                    nc.tensor.matmul(row_ps[:, P:2 * P], ones[:, :], recv_diag[:, :], start=True, stop=True)\
                      .then_inc(tile_tensor, 1)
                    tile_step(pe, tile_vector, VECTOR_STEPS, i, "embedding")
                    nc.tensor.matmul(hid_ps[0][:, 0:P], w0_groups[:, 0, :, :].rearrange("p s f -> p (s f)"),
                                     emb[:, 0:P], start=True, stop=True).then_inc(tile_tensor, 1)
                    tile_step(pe, tile_scalar, SCALAR_STEPS, i, "hidden0")
                    nc.tensor.matmul(hid_ps[1][:, 0:P], w1_diag[:, :], h1[:, 0:P], start=True, stop=True)\
                      .then_inc(tile_tensor, 1)
                    tile_step(pe, tile_scalar, SCALAR_STEPS, i, "hidden1")
                    nc.tensor.matmul(w_ps[0][:, 0:P], ones_bf[:, :], b2_rows[:, 0, :], start=True, stop=False)
                    nc.tensor.matmul(w_ps[0][:, 0:P], h2[0][:, 0:P], w2_diag[:, 0:P], start=False, stop=True)\
                      .then_inc(tile_tensor, 1)
                    tile_step(pe, tile_vector, VECTOR_STEPS, i, "dot_block")
                    for j in range(2):
                        last = nc.tensor.matmul(upd_ps[:, j * P:(j + 1) * P], msg[0][:, 0, j * P:(j + 1) * P],
                                                same[:, :], start=True, stop=True)
                    last.then_inc(tile_tensor, 1)
                    tile_step(pe, tile_scalar, SCALAR_STEPS, i, "placed")
                    for j in range(2):
                        last = nc.tensor.matmul(upd_ps[:, 2 * P:3 * P], nodesT[:, j * P:(j + 1) * P],
                                                wout[:, j, :], start=j == 0, stop=j == 1)
                    last.then_inc(tile_tensor, 1)

        @block.scalar
        def _(act):
            def load_x(g, ring):
                r = x[bass.ds(g * NG * P, NG * P), :].rearrange("(t p) f -> p t f", p=P)
                act.dma_start(x_ring[:, ring, :, :], r).then_inc(x_loaded[ring], 16)

            def reload_x(g, ring):
                act.wait_ge(xT_ready, g + 1)
                load_x(g + RING, ring)

            def copy_projected(g, ring, saves=None):
                act.wait_ge(proj_ready, g + 1)
                if saves is not None:
                    act.wait_ge(proj_saved[ring], 16 * saves)
                nc.scalar.activation(proj[:, ring, :], w_ps[ring % 2][:, :], ACT.Copy).then_inc(proj_copied, 1)

            for ring in range(RING):
                load_x(ring, ring)
            for ring in range(RING):
                reload_x(ring, ring)
                copy_projected(ring, ring)
            with act.Fori(1, NODE_GROUPS // RING - 1) as k:
                for ring in range(RING):
                    g = RING * k + ring
                    reload_x(g, ring)
                    copy_projected(g, ring, k)
            k = NODE_GROUPS // RING - 1
            for ring in range(RING):
                if ring == 0:
                    row = NODE_GROUPS * NG * P
                    act.wait_ge(xT_ready, RING * k + 1)
                    act.dma_start(x_ring[:, 0, 0, :], x[row:row + P, :]).then_inc(x_loaded[0], 16)
                    act.dma_start(x_ring[0:LAST_NODES, 0, 1, :], x[row + P:NODES, :]).then_inc(x_loaded[0], 16)
                copy_projected(RING * k + ring, ring, k)
            act.wait_ge(proj_ready, NODE_GROUPS + 1)
            act.wait_ge(proj_saved[0], 16 * (NODE_GROUPS // RING))
            nc.scalar.activation(proj[:, 0, 0:P], w_ps[0][:, 0:P], ACT.Copy)
            nc.scalar.activation(proj[0:LAST_NODES, 0, P:2 * P], w_ps[0][0:LAST_NODES, P:2 * P], ACT.Copy)\
              .then_inc(proj_copied, 1)
            act.wait_ge(const_step, WUP)

            def copy_windows(c):
                act.wait_ge(msg_summed, 2 * (c + 1))
                nc.scalar.activation(win_sb[:, :], win_ps[:, 0:MSG], ACT.Copy).then_inc(win_copied, 1)

            def gaussians(c):
                act.wait_ge(clip_ready, c + 1)
                nc.scalar.activation(gauss_arg[:, :], r_clip[:, :], ACT.Square, bias=minus_center[:, 0:1],
                                     scale=float(CENTERS - 1)).then_inc(gauss_step, 1)
                act.wait_ge(gauss_step, 2 * c + 1)
                nc.scalar.activation(gauss[:, :], gauss_arg[:, :], ACT.Exp, scale=-0.5).then_inc(gauss_step, 1)

            def edge_norms(c):
                act.wait_ge(clip_ready, c + 1)
                nc.scalar.activation(square[:, :, :], row_ps[:, 2 * V:5 * V].rearrange("p (c v) -> p c v", c=3),
                                     ACT.Square).then_inc(squared, 1)
                act.wait_ge(norm2_ready, c + 1)
                nc.scalar.activation(norm[:, :], norm2[:, :], ACT.Sqrt).then_inc(norm_ready, 1)

            def silus(c, b):
                for n in range(8):
                    act.wait_ge(hid_ready, 8 * c + n + 1)
                    layer, i = divmod(n, 4)
                    to = h1 if layer == 0 else h2[b]
                    nc.scalar.activation(to[:, i * HCOL:(i + 1) * HCOL], hid_ps[n % 2][:, 0:HCOL], ACT.Silu,
                                         bias=bias01[:, layer:layer + 1]).then_inc(hid_copied, 1)

            def copy_weights(k, b, at, h):
                c = 2 * k + b
                if from_chunk(at, 1):
                    act.wait_ge(msg_ready, 2 * (c - 1) + h + 1)
                for i in range(W_GROUPS):
                    m = h * W_GROUPS + i
                    n = min(4, HALF_V - 4 * i)
                    act.wait_ge(w_ready, 8 * c + m + 1)
                    nc.scalar.activation(w_edge[h][:, 4 * i:4 * i + n, :],
                                         w_ps[m % 2][:, 0:n * P].rearrange("p (v f) -> p v f", f=P),
                                         ACT.Copy).then_inc(w_copied, 1)

            def copy_placed(c):
                act.wait_ge(placed, c + 1)
                nc.scalar.activation(nodesT[:, :], upd_ps[:, 0:MSG], ACT.Copy).then_inc(placed_copied, 1)

            def chunk(k, b, at, norms):
                c = 2 * k + b
                nxt = after(k, b)
                at_next = None if at is None else at + 1
                if from_chunk(at, 1):
                    copy_windows(c - 1)
                if has_next(at):
                    edge_norms(c + 1)
                    gaussians(c + 1)
                copy_weights(k, b, at, 1)
                if from_chunk(at, 1):
                    copy_placed(c - 1)
                if has_next(at):
                    silus(c + 1, nxt[1])
                    copy_weights(*nxt, at_next, 0)
                if norms:
                    deviation(turn_ln, c - LAG)

            def deviation(signals, n):
                act.wait_ge(signals[1], n + 1)
                nc.scalar.activation(ln_sd[:, :], ln_var[:, :], ACT.Sqrt).then_inc(signals[2], 1)

            edge_norms(0)
            gaussians(0)
            act.wait_ge(const_step, CONST_STEPS)
            silus(0, 0)
            copy_weights(0, 0, 0, 0)
            each_chunk(act, chunk)
            copy_windows(CHUNKS - 1)
            copy_placed(CHUNKS - 1)

            act.wait_ge(flag_ready, 1)
            with act.If(act.value_load(flag[0:1, 0:1], min_val=0, max_val=P) > 0):
                with act.Fori(0, EDGE_TILES) as i:
                    act.wait_ge(tile_loaded, 16 * TILE_LOADS * i + 16 * TILE_LOADS)
                    nc.scalar.activation(one_square[:, :], one_attr[:, :], ACT.Square).then_inc(tile_scalar, 1)
                    tile_step(act, tile_vector, VECTOR_STEPS, i, "clip")
                    nc.scalar.activation(gauss_arg[:, 0:P], r_clip[:, 0:P], ACT.Square, bias=minus_center[:, 0:1],
                                         scale=float(CENTERS - 1)).then_inc(tile_scalar, 1)
                    tile_step(act, tile_scalar, SCALAR_STEPS, i, "gauss_arg")
                    nc.scalar.activation(gauss[:, 0:P], gauss_arg[:, 0:P], ACT.Exp, scale=-0.5)\
                      .then_inc(tile_scalar, 1)
                    tile_step(act, tile_vector, VECTOR_STEPS, i, "norm2")
                    nc.scalar.activation(one_norm[:, 2:3], one_norm[:, 1:2], ACT.Sqrt).then_inc(tile_scalar, 1)
                    for layer, (name, to) in enumerate((("hidden0", h1), ("hidden1", h2[0]))):
                        tile_step(act, tile_tensor, TENSOR_STEPS, i, name)
                        nc.scalar.activation(to[:, 0:P], hid_ps[layer][:, 0:P], ACT.Silu,
                                             bias=bias01[:, layer:layer + 1]).then_inc(tile_scalar, 1)
                    tile_step(act, tile_tensor, TENSOR_STEPS, i, "weights")
                    nc.scalar.activation(w_edge[0][:, 0, :], w_ps[0][:, 0:P], ACT.Copy).then_inc(tile_scalar, 1)
                    tile_step(act, tile_tensor, TENSOR_STEPS, i, "placed")
                    nc.scalar.activation(nodesT[:, :], upd_ps[:, 0:MSG], ACT.Copy).then_inc(tile_scalar, 1)

            with act.If(act.value_load(flag[0:1, 1:2], min_val=0, max_val=P) > 0):
                with act.Fori(0, EARLY) as i:
                    deviation(again_ln, i)
            for i in range(TAIL):
                deviation(tail_ln, i)

        @block.vector
        def _(dve):
            n_dve = [0]

            def step(ins):
                ins.then_inc(const_step, 1)
                n_dve[0] += 1
                return n_dve[0]

            def settle():
                dve.wait_ge(const_step, n_dve[0])

            def edge_rows(k, b, at):
                c = 2 * k + b
                dve.wait_ge(rows_loaded[b], loaded_count(k, at))
                if from_chunk(at, 1):
                    dve.wait_ge(transposed, c)
                nc.vector.tensor_copy(src_f[:, :], src_row[b][:, :])
                nc.vector.tensor_copy(chunk_start[b][:, :], base[b][:, 1:2]).then_inc(start_known, 1)
                nc.vector.tensor_scalar(rel[:, :], dst_row[b][:, :], base[b][:, 0:1], None, ALU.subtract)\
                  .then_inc(rows_ready, 1)
                nc.vector.scalar_tensor_tensor(window_node[b][:, :], base[b][:, 0:1], window_lane[:, 0:1],
                                               base[b][:, 1:2], ALU.add, ALU.subtract).then_inc(edge_scalars, 1)

            def leftovers(k, b, at):
                c = 2 * k + b
                nc.vector.tensor_scalar(chunk_rel[:, :], dst_row[b][:, :], base[b][:, 1:2], None, ALU.subtract)\
                  .then_inc(left_step, 1)
                nc.vector.tensor_tensor(above_trash[:, :], dst_row[b][:, :], trash_row[:, :], ALU.subtract)\
                  .then_inc(left_step, 1)
                dve.wait_ge(rows_ready, c + 1)
                nc.vector.scalar_tensor_tensor(window_out[:, :], rel[:, :], float(1 - WINDOW), rel[:, :],
                                               ALU.add, ALU.mult).then_inc(left_step, 1)
                dve.wait_ge(left_step, 7 * c + 1)
                nc.vector.scalar_tensor_tensor(chunk_out[:, :], chunk_rel[:, :], float(1 - P), chunk_rel[:, :],
                                               ALU.add, ALU.mult).then_inc(left_step, 1)
                dve.wait_ge(left_step, 7 * c + 4)
                nc.vector.tensor_tensor(missed[:, :], window_out[:, :], chunk_out[:, :], ALU.max)\
                  .then_inc(left_step, 1)
                dve.wait_ge(left_step, 7 * c + 5)
                nc.vector.scalar_tensor_tensor(missed_row[:, :], missed[:, :], 0.0, above_trash[:, :],
                                               ALU.is_gt, ALU.mult).then_inc(left_step, 1)
                full = at != CHUNKS - 1
                for p0, n in ((0, P),) if full else ((0, T), (WINDOW, LAST_B)):
                    last = nc.vector.tensor_tensor(missed_any[p0:p0 + n, :], missed_any[p0:p0 + n, :],
                                                   missed[p0:p0 + n, :], ALU.max)
                last.then_inc(left_step, 1)
                dve.wait_ge(left_step, 7 * c + 7)
                if from_chunk(at, 2):
                    dve.wait_ge(left_saved[b], 32 * k)
                nc.vector.tensor_tensor(left_row[b][:, :], missed_row[:, :], trash_row[:, :], ALU.add)\
                  .then_inc(left_ready, 1)

            for tile in (wup_raw[:, :], w1_diag[:, :], w2_diag[:, :], wout[:, :, :], zeros[:, :],
                         src_row[0][:, :], src_row[1][:, :], dst_row[0][:, :], dst_row[1][:, :]):
                nc.vector.memset(tile, 0)
            for b in range(2):
                nc.vector.memset(attr_row[b][:, :, :], 0.0)
                nc.vector.memset(r_in[b][:, :], 0.0)
            nc.vector.memset(ones[:, :], 1.0)
            step(nc.vector.memset(missed_any[:, :], 0.0))
            nc.vector.memset(reach_back[:, :], 0.0)
            nc.vector.memset(normed_end[:, :], float(P)).then_inc(reach_step, 1)
            nc.vector.memset(ones_bf[:, :], 1.0)
            nc.vector.memset(wout_scale[:, :], 1.0 / 128)
            dve.wait_ge(const_pool, 2)
            step(nc.vector.tensor_copy(iota_f[:, :], iota_i[:, :]))
            step(nc.vector.tensor_copy(pcol[:, :], pcol_i[:, 0:1]))
            step(nc.vector.tensor_single_scalar(pcol_i[:, 1:2], pcol_i[:, 0:1], WINDOW - 1, op=ALU.bitwise_and))
            step(nc.vector.tensor_single_scalar(pcol_i[:, 2:3], pcol_i[:, 0:1], CENTERS - 1, op=ALU.bitwise_and))
            settle()
            for half, p0 in ((0, 64), (1, 0), (1, 64)):
                nc.vector.memset(wout_scale[p0:p0 + MUL, half:half + 1], math.sqrt(3.0) / 128)
            step(nc.vector.tensor_scalar(trash_row[:, :], iota_f[:, :], float(NODES), None, ALU.add))
            step(nc.vector.tensor_copy(window_lane[:, :], pcol_i[:, 1:2]))
            step(nc.vector.tensor_scalar(minus_center[:, :], pcol_i[:, 2:3], -1.0, None, ALU.mult))
            step(nc.vector.tensor_single_scalar(lane_center_i[:, :], iota_i[:, :], CENTERS - 1, op=ALU.bitwise_and))
            settle()
            step(nc.vector.tensor_copy(lane_center[:, :], lane_center_i[:, :]))
            settle()
            step(nc.vector.tensor_scalar(center_rows[:, :], lane_center[0:CENTERS, :], pcol[0:CENTERS, 0:1], None,
                                         ALU.is_equal))

            def copy_xT(g, half, first=False, n=NG * P):
                dve.wait_ge(xT_ready, g + 1)
                if not first:
                    dve.wait_ge(proj_ready, g - 1)
                nc.vector.tensor_copy(xT[:, half, 0:n], hid_ps[half][:, 0:n]).then_inc(xT_copied, 1)

            for ring in range(RING):
                copy_xT(ring, ring % 2, first=ring < 2)
                if ring == 1:
                    dve.wait_ge(wup_loaded, 64)
                    assert step(nc.vector.tensor_scalar(wup[:, :], wup_raw[:, :], 1.0 / math.sqrt(MUL), None,
                                                        ALU.mult)) == WUP
            settle()
            edge_rows(0, 0, 0)
            dve.wait_ge(w0_repeated, 1)
            assert step(nc.vector.tensor_scalar(
                w0_wide[:, :, :, :].rearrange("p q s f -> p (q s) f"), spread(win_ps[:, 0:HID], 1, 16),
                math.sqrt(CENTERS), None, ALU.mult)) == W0_WIDE
            with dve.Fori(1, NODE_GROUPS // RING) as k:
                for ring in range(RING):
                    copy_xT(RING * k + ring, ring % 2)
            copy_xT(NODE_GROUPS, 0, n=(SHORT - 1) * P + LAST_NODES)

            def edge_columns(k, b, at):
                c = 2 * k + b
                dve.wait_ge(transposed, c + 1)
                if from_chunk(at, 2):
                    dve.wait_ge(gathered[b][1], 16 * HALF_V * k)
                nc.vector.tensor_copy(idx[b][:, :], row_ps[:, 0:V]).then_inc(idx_ready, 1)
                nc.vector.tensor_scalar(r_clip[:, :], row_ps[:, 5 * V:5 * V + GROUP], 0.0, 1.0, ALU.max, ALU.min)\
                  .then_inc(clip_ready, 1)
                dve.wait_ge(squared, c + 1)
                nc.vector.tensor_tensor(norm_a[:, :], square[:, 0, :], square[:, 1, :], ALU.add).then_inc(norm_step, 1)
                dve.wait_ge(norm_step, 3 * c + 1)
                nc.vector.tensor_tensor(norm2[:, :], norm_a[:, :], square[:, 2, :], ALU.add).then_inc(norm2_ready, 1)
                if from_chunk(at, 2):
                    dve.wait_ge(msg_summed, 2 * (c - 1))
                nc.vector.tensor_tensor(one_hot[b][:, :, :], spread(iota_f[:, 0:WINDOW], 1, V),
                                        spread(row_ps[:, V:2 * V], 2, WINDOW), ALU.is_equal)\
                  .then_inc(one_hot_ready, 1)
                dve.wait_ge(norm_ready, c + 1)
                nc.vector.tensor_scalar(norm_eps[:, :], norm[:, :], 1e-12, None, ALU.add).then_inc(norm_step, 1)
                dve.wait_ge(gauss_step, 2 * c + 2)
                if from_chunk(at, 1):
                    dve.wait_ge(hid_ready, 8 * c - 4)
                nc.vector.scalar_tensor_tensor(emb[:, :], row_ps[:, 5 * V:5 * V + GROUP], 1.0, gauss[:, :], ALU.is_le, ALU.mult)\
                  .then_inc(emb_ready, 1)
                dve.wait_ge(norm_step, 3 * c + 2)
                nc.vector.reciprocal(norm_inv[:, :], norm_eps[:, :]).then_inc(norm_step, 1)
                dve.wait_ge(norm_step, 3 * c + 3)
                nc.vector.tensor_tensor(unit[b][:, :, :], row_ps[:, 2 * V:5 * V].rearrange("p (c v) -> p c v", c=3),
                                        spread(norm_inv[:, :], 1, 3), ALU.mult).then_inc(unit_ready, 1)

            def window_place(k, b, at):
                c = 2 * k + b
                if from_chunk(at, 2):
                    dve.wait_ge(placed, c - 1)
                dve.wait_ge(edge_scalars, c + 1)
                nc.vector.tensor_scalar(place[b][:, :], iota_f[:, :], window_node[b][:, 0:1], None, ALU.is_equal)\
                  .then_inc(place_ready, 1)

            def messages(k, b, at, h, part=0):
                c = 2 * k + b
                n = 2 * c + h
                in_parts = at == CHUNKS - 1 and h == 1
                v0, v1, stride = END_PARTS[part] if in_parts else (0, HALF_V, 1)
                tiles = slice(v0, v1, stride)
                if part == 1:
                    dve.wait_ge(end_gathered, 16 * len(range(v0, v1, stride)))
                elif in_parts:
                    dve.wait_ge(gathered[b][h], 16 * HALF_V * k + 16 * len(range(v0, v1, stride)))
                else:
                    dve.wait_ge(gathered[b][h], 16 * HALF_V * k + 16 * len(last_tiles(at, h)))
                dve.wait_ge(unit_ready, c + 1)
                dve.wait_ge(w_copied, 4 * n + 4)
                m_blocks = msg[h][:, tiles, :].rearrange("p v (k f) -> p v k f", f=MUL)
                w_blocks = w_edge[h][:, tiles, :].rearrange("p v (k f) -> p v k f", f=MUL)
                xs = rows[b][h][:, tiles, 0:MUL]
                xv = rows[b][h][:, tiles, MUL:FEAT].rearrange("p v (c f) -> p v c f", f=MUL)
                y = unit[b][:, :, h * HALF_V + v0:h * HALF_V + v1:stride].rearrange("p c v -> p v c")
                nc.vector.tensor_tensor(dot[:, tiles, :, :], xv, spread(y, 3, MUL), ALU.mult).then_inc(msg_step, 1)
                if from_chunk(at, 1):
                    dve.wait_ge(msg_summed, n - 1)
                nc.vector.tensor_tensor(m_blocks[:, :, 0:9:8, :], w_blocks[:, :, 0:2, :], spread(xs, 2, 2), ALU.mult)\
                  .then_inc(msg_step, 1)
                nc.vector.tensor_tensor(m_blocks[:, :, 3:8:2, :], spread(w_blocks[:, :, 2, :], 2, 3), xv, ALU.mult)\
                  .then_inc(msg_step, 1)
                dve.wait_ge(msg_step, 5 * (n + part) + 2)
                nc.vector.tensor_tensor(dot_a[:, tiles, :], dot[:, tiles, 0, :], dot[:, tiles, 1, :], ALU.add).then_inc(msg_step, 1)
                nc.vector.tensor_tensor(m_blocks[:, :, 2:7:2, :], spread(m_blocks[:, :, 8, :], 2, 3),
                                        spread(y, 3, MUL), ALU.mult)
                dve.wait_ge(msg_step, 5 * (n + part) + 4)
                nc.vector.tensor_tensor(dot_b[:, tiles, :], dot_a[:, tiles, :], dot[:, tiles, 2, :], ALU.add).then_inc(msg_step, 1)
                dve.wait_ge(msg_step, 5 * (n + part) + 5)
                nc.vector.tensor_tensor(m_blocks[:, :, 1, :], dot_b[:, tiles, :], w_blocks[:, :, 3, :], ALU.mult)\
                  .then_inc(msg_ready, 1)

            def add_window(c):
                dve.wait_ge(upd_ready, c + 1)
                dve.wait_ge(window_read, 16 * (c + 1))
                nc.vector.tensor_tensor(new_sum[:, :], upd_ps[:, 2 * P:3 * P], old_sum[:, :], ALU.add)\
                  .then_inc(window_added, 1)

            def chunk(k, b, at, norms):
                nxt = after(k, b)
                at_next = None if at is None else at + 1
                if has_next(at):
                    edge_rows(*nxt, at_next)
                    leftovers(*nxt, at_next)
                    edge_columns(*nxt, at_next)
                window_place(k, b, at)
                messages(k, b, at, 0)
                if from_chunk(at, 1):
                    add_window(2 * k + b - 1)
                messages(k, b, at, 1)
                if at == CHUNKS - 1:
                    messages(k, b, at, 1, part=1)
                if norms:
                    reach(k, b)
                    dve.wait_ge(ln_loaded[b], 16 * (k - LAG // 2 + 1))
                    normalize(ln_in[b], ln_out[b], turn_ln, 2 * k + b - LAG)

            def reach(k, b):
                c = 2 * k + b
                dve.wait_ge(start_known, c + 1)
                n = c - LAG
                dve.wait_ge(reach_step, 3 * n + 1)
                nc.vector.tensor_tensor(reach_back[:, 0:1], normed_end[:, :], chunk_start[b][:, :],
                                        ALU.subtract).then_inc(reach_step, 1)
                dve.wait_ge(reach_step, 3 * n + 2)
                nc.vector.tensor_tensor(reach_back[:, 1:2], reach_back[:, 1:2], reach_back[:, 0:1], ALU.max)\
                  .then_inc(reach_step, 1)
                nc.vector.tensor_scalar(normed_end[:, :], normed_end[:, :], float(P), None, ALU.add)\
                  .then_inc(reach_step, 1)

            def normalize(rows_in, rows_out, signals, n):
                stats, variance, deviation, inverse, result = signals
                nc.vector.bn_stats(ln_stat[:, :], rows_in[:, :]).then_inc(stats, 1)
                dve.wait_ge(stats, 3 * n + 1)
                dve.sem_inc(stats, 1)
                nc.vector.bn_aggr(ln_mv[:, :], ln_stat[:, :]).then_inc(stats, 1)
                dve.wait_ge(stats, 3 * n + 3)
                nc.vector.tensor_scalar(ln_var[:, :], ln_mv[:, 1:2], 1e-5, None, ALU.add).then_inc(variance, 1)
                dve.wait_ge(deviation, n + 1)
                nc.vector.reciprocal(ln_rs[:, :], ln_sd[:, :]).then_inc(inverse, 1)
                dve.wait_ge(inverse, n + 1)
                nc.vector.tensor_scalar(rows_out[:, :], rows_in[:, :], ln_mv[:, 0:1], ln_rs[:, 0:1], ALU.subtract,
                                        ALU.mult).then_inc(result, 1)

            edge_columns(0, 0, 0)
            dve.wait_ge(const_loaded, 16 * CONST_DMAS)
            step(nc.vector.tensor_copy(b2_part[:, 0, :], b2_rep[:, :]))
            settle()
            step(nc.vector.tensor_tensor(b2_rest[:, 0, :], b2_rep[:, :], b2_part[:, 0, :], ALU.subtract))
            settle()
            step(nc.vector.tensor_copy(b2_part[:, 1, :], b2_rest[:, 0, :]))
            settle()
            step(nc.vector.tensor_tensor(b2_rest[:, 1, :], b2_rest[:, 0, :], b2_part[:, 1, :], ALU.subtract))
            for i in range(3):
                step(nc.vector.tensor_scalar(b2_mask[:, i:i + 1], pcol[:, :], float(i), None, ALU.is_equal))
            settle()
            step(nc.vector.tensor_copy(b2_part[:, 2, :], b2_rest[:, 1, :]))
            step(nc.vector.tensor_scalar(b2_sum[:, 0, :], b2_part[:, 0, :], b2_mask[:, 0:1], None, ALU.mult))
            settle()
            step(nc.vector.scalar_tensor_tensor(b2_sum[:, 1, :], b2_part[:, 1, :], b2_mask[:, 1:2],
                                                b2_sum[:, 0, :], ALU.mult, ALU.add))
            settle()
            step(nc.vector.scalar_tensor_tensor(b2_rows[:, :, :], spread(b2_part[:, 2, :], 1, 4), b2_mask[:, 2:3],
                                                spread(b2_sum[:, 1, :], 1, 4), ALU.mult, ALU.add))
            step(nc.vector.tensor_scalar(wout[0:HID, 0, 0:MUL], wout_raw[0:HID, 0, :], wout_scale[0:HID, 0:1],
                                         None, ALU.mult))
            for half, p0, c in ((0, HID, 0), (1, 0, 1), (1, HID, 2)):
                step(nc.vector.tensor_scalar(wout[p0:p0 + HID, half, MUL + c:MUL + c + 3 * (MUL - 1) + 1:3],
                                             wout_raw[p0:p0 + HID, half, :], wout_scale[p0:p0 + HID, half:half + 1],
                                             None, ALU.mult))
            assert n_dve[0] == CONST_STEPS, n_dve[0]
            settle()
            leftovers(0, 0, 0)
            each_chunk(dve, chunk)
            nc.vector.tensor_reduce(valid_row[:, :], row_select[:, :], AX.X, ALU.add).then_inc(flag_step, 1)
            dve.wait_ge(left_ready, CHUNKS)
            dve.wait_ge(reach_step, 3 * EARLY + 1)
            nc.vector.tensor_reduce(missed_col[:, 0:1], missed_any[:, :], AX.X, ALU.max).then_inc(flag_step, 1)
            nc.vector.tensor_scalar(missed_col[:, 3:4], reach_back[:, 1:2], 0.0, None, ALU.is_gt)\
              .then_inc(flag_step, 1)
            dve.wait_ge(flag_step, 3)
            nc.vector.tensor_scalar(missed_col[:, 1:2], missed_col[:, 0:1], 0.0, None, ALU.is_gt)\
              .then_inc(flag_step, 1)
            dve.wait_ge(flag_step, 4)
            nc.vector.tensor_tensor(missed_col[:, 2:3], missed_col[:, 1:2], missed_col[:, 3:4], ALU.max)\
              .then_inc(flag_step, 1)
            dve.wait_ge(flag_summed, 1)
            nc.vector.tensor_copy(flag[0:1, 0:2], row_ps[0:1, 0:2]).then_inc(flag_ready, 1)
            add_window(CHUNKS - 1)
            dve.wait_ge(flag_ready, 1)

            with dve.If(dve.value_load(flag[0:1, 0:1], min_val=0, max_val=P) > 0):
                with dve.Fori(0, EDGE_TILES) as i:
                    def vector_step(ins):
                        ins.then_inc(tile_vector, 1)

                    def made(name):
                        tile_step(dve, tile_vector, VECTOR_STEPS, i, name)

                    tile_step(dve, tile_tensor, TENSOR_STEPS, i, "lengths")
                    vector_step(nc.vector.tensor_scalar(r_clip[:, 0:P], row_ps[:, 0:P], 0.0, 1.0, ALU.max, ALU.min))
                    tile_step(dve, tile_scalar, SCALAR_STEPS, i, "gauss")
                    vector_step(nc.vector.scalar_tensor_tensor(emb[:, 0:P], row_ps[:, 0:P], 1.0, gauss[:, 0:P],
                                                               ALU.is_le, ALU.mult))
                    vector_step(nc.vector.tensor_tensor(one_norm[:, 0:1], one_square[:, 0:1], one_square[:, 1:2],
                                                        ALU.add))
                    made("norm_a")
                    vector_step(nc.vector.tensor_tensor(one_norm[:, 1:2], one_norm[:, 0:1], one_square[:, 2:3],
                                                        ALU.add))
                    tile_step(dve, tile_scalar, SCALAR_STEPS, i, "norm")
                    vector_step(nc.vector.tensor_scalar(one_norm[:, 3:4], one_norm[:, 2:3], 1e-12, None, ALU.add))
                    made("norm_eps")
                    vector_step(nc.vector.reciprocal(one_norm[:, 4:5], one_norm[:, 3:4]))
                    made("norm_inv")
                    vector_step(nc.vector.tensor_scalar(one_unit[:, :], one_attr[:, :], one_norm[:, 4:5], None,
                                                        ALU.mult))
                    dve.wait_ge(tile_loaded, 16 * TILE_LOADS * i + 16 * TILE_LOADS)
                    vector_step(nc.vector.tensor_copy(recv[:, :], one_left[:, :]))
                    made("recv")
                    vector_step(nc.vector.tensor_scalar(recv_diag[:, :], ident[:, :], recv[:, 0:1], None, ALU.mult))
                    tile_step(dve, tile_tensor, TENSOR_STEPS, i, "receivers")
                    vector_step(nc.vector.tensor_scalar(same[:, :], row_ps[:, P:2 * P], recv[:, 0:1], None,
                                                        ALU.is_equal))
                    made("same")
                    vector_step(nc.vector.tensor_tensor(same_earlier[:, :], same[:, :], earlier[:, :], ALU.mult))
                    made("same_earlier")
                    vector_step(nc.vector.tensor_reduce(repeated[:, 0:1], same_earlier[:, :], AX.X, ALU.max))
                    made("repeated")
                    vector_step(nc.vector.scalar_tensor_tensor(repeated[:, 1:2], pcol[:, :], float(NODES),
                                                               recv[:, :], ALU.add, ALU.subtract))
                    made("keep_first")
                    vector_step(nc.vector.scalar_tensor_tensor(target[:, :], repeated[:, 1:2], repeated[:, 0:1],
                                                               recv[:, :], ALU.mult, ALU.add))
                    dve.wait_ge(tile_rows, 16 * i + 16)
                    tile_step(dve, tile_scalar, SCALAR_STEPS, i, "weights")
                    m = msg[0][:, 0, :].rearrange("p (k f) -> p k f", f=MUL)
                    w = w_edge[0][:, 0, :].rearrange("p (k f) -> p k f", f=MUL)
                    xs = rows[0][0][:, 0, 0:MUL]
                    xv = rows[0][0][:, 0, MUL:FEAT].rearrange("p (c f) -> p c f", f=MUL)
                    y = spread(one_unit[:, :], 2, MUL)
                    vector_step(nc.vector.tensor_tensor(dot[:, 0, :, :], xv, y, ALU.mult))
                    vector_step(nc.vector.tensor_tensor(m[:, 0:9:8, :], w[:, 0:2, :], spread(xs, 1, 2), ALU.mult))
                    vector_step(nc.vector.tensor_tensor(m[:, 3:8:2, :], spread(w[:, 2, :], 1, 3), xv, ALU.mult))
                    made("scalar_blocks")
                    vector_step(nc.vector.tensor_tensor(dot_a[:, 0, :], dot[:, 0, 0, :], dot[:, 0, 1, :], ALU.add))
                    vector_step(nc.vector.tensor_tensor(m[:, 2:7:2, :], spread(m[:, 8, :], 1, 3), y, ALU.mult))
                    made("dot_a")
                    vector_step(nc.vector.tensor_tensor(dot_b[:, 0, :], dot_a[:, 0, :], dot[:, 0, 2, :], ALU.add))
                    made("dot_b")
                    vector_step(nc.vector.tensor_tensor(m[:, 1, :], dot_b[:, 0, :], w[:, 3, :], ALU.mult))
                    tile_step(dve, tile_tensor, TENSOR_STEPS, i, "update")
                    dve.wait_ge(tile_sums, 16 * i + 16)
                    vector_step(nc.vector.tensor_tensor(new_sum[:, :], upd_ps[:, 2 * P:3 * P], old_sum[:, :],
                                                        ALU.add))

            with dve.If(dve.value_load(flag[0:1, 1:2], min_val=0, max_val=P) > 0):
                with dve.Fori(0, EARLY) as i:
                    dve.wait_ge(again_loaded, 16 * i + 16)
                    normalize(ln_in[0], ln_out[0], again_ln, i)
            dve.wait_ge(tail_loaded, 16 * TAIL)
            for i in range(TAIL):
                normalize(ln_in[i], ln_out[i], tail_ln, i)


CONST_DMAS = 13
WUP = 12
W0_WIDE = 13
CONST_STEPS = 28

_INS = ["x", "src", "dst", "edge_attr_3", "edge_weight"] + [
    "L0_gnn_" + n for n in ("W_up0", "W_up1", "mlp_w0", "mlp_b0", "mlp_w1", "mlp_b1", "mlp_w2", "mlp_b2",
                            "W_out0", "W_out1")]


def kernel(**inputs):
    import numpy as np
    import concourse.bacc as bacc
    from concourse.bass_utils import run_bass_kernel_spmd as run

    nc = bacc.Bacc("TRN2", target_bir_lowering=False, num_devices=1)
    arrays, args = {}, []
    for name in _INS:
        a = np.ascontiguousarray(inputs[name])
        arrays[f"in_{name}"] = a
        args.append(nc.dram_tensor(f"in_{name}", a.shape, mybir.dt.from_np(a.dtype), kind="ExternalInput").ap())
    out = nc.dram_tensor("out_nodes", (NODES, FEAT), F32, kind="ExternalOutput").ap()
    build(nc, *args, out)
    r = run(nc, [arrays], core_ids=[0])
    return r.results[0]["out_nodes"]
```
